# Optimizing a Trainium2 kernel written in Bass

```python
import numpy as np
import jax
import jax.numpy as jnp

def _softmax(x, axis=-1):
    return jax.nn.softmax(x, axis=axis)

def _gelu(x):
    return jax.nn.gelu(x, approximate=True)

def _silu(x):
    return jax.nn.silu(x)

def _sigmoid(x):
    return jax.nn.sigmoid(x)

def _layernorm(x, axis=-1, eps=1e-05):
    m = jnp.mean(x, axis=axis, keepdims=True)
    v = jnp.var(x, axis=axis, keepdims=True)
    return (x - m) / jnp.sqrt(v + eps)

def _scatter_add(tgt, idx, src, axis=0):
    return tgt.at[idx].add(src)

def _segment_sum(src, seg, n):
    return jax.ops.segment_sum(src, seg, n)
kernel_name = 'mk_adj_preln_d4_adj_r2_c3e806'

def setup_inputs(seed: int=0):
    np.random.seed(seed)
    _w = jnp.asarray

    def _rec_inputs():
        import jax
        import jax.numpy as jnp
        _gk = jax.random.key(seed)
        x = -0.0002928 + 1 * jax.random.normal(jax.random.fold_in(_gk, 1), (128, 128, 128), jnp.float32)
        _a = jax.random.bernoulli(jax.random.fold_in(_gk, 2), 0.03125, (128, 128, 128))
        _a = jnp.logical_or(_a, jnp.swapaxes(_a, -1, -2))
        _a = jnp.logical_or(_a, jnp.eye(128, dtype=bool))
        _af = _a.astype(jnp.float32)
        _af = _af * jax.random.uniform(jax.random.fold_in(_gk, 3), (128, 128, 128), jnp.float32, 0.05, 0.999994)
        adj = _af
        _nm = jnp.ones((128, 128), dtype=bool)
        nodemask = jnp.where(_nm, 1.0, 0.0).astype(jnp.float32)
        return (x, adj, nodemask)
    x, adj, nodemask = _rec_inputs()

    def _L0_gnn_setup():
        import jax, jax.numpy as jnp
        import numpy as np
        EPS = 1e-08
        key = jax.random.key(seed)
        kH, kA, kW = jax.random.split(key, 3)
        B, N, IN, OUT = (32, 256, 128, 128)
        H = jax.random.normal(kH, (B, N, IN), dtype=jnp.float32)
        A = jax.random.uniform(kA, (B, N, N), dtype=jnp.float32)
        mask = jnp.ones((B, N), dtype=jnp.float32)
        W = jax.random.normal(kW, (OUT, IN), dtype=jnp.float32) * (1.0 / np.sqrt(IN))
        b = jnp.zeros((OUT,), dtype=jnp.float32)
        return {'H': H, 'A': A, 'mask': mask, 'W': W, 'b': b}
    _L0_gnn_all = _L0_gnn_setup()
    _L0_gnn_in = {k: v for k, v in _L0_gnn_all.items() if k in ('W', 'b')}
    del _L0_gnn_all

    def _L1_gnn_setup():
        import jax, jax.numpy as jnp
        import numpy as np
        LN_EPS = 1e-05
        key = jax.random.key(seed)
        k1, k2, k3, k4 = jax.random.split(key, 4)
        B, N, F, O = (8, 1024, 128, 128)
        x = jax.random.normal(k1, (B, N, F), dtype=jnp.float32)
        adj = jax.random.uniform(k2, (B, N, N), dtype=jnp.float32)
        gamma = jnp.ones((F,), jnp.float32)
        beta = jnp.zeros((F,), jnp.float32)
        W_self = jax.random.normal(k3, (F, O), dtype=jnp.float32) * (1.0 / np.sqrt(F))
        W_neigh = jax.random.normal(k4, (F, O), dtype=jnp.float32) * (1.0 / np.sqrt(F))
        return {'x': x, 'adj': adj, 'gamma': gamma, 'beta': beta, 'W_self': W_self, 'W_neigh': W_neigh}
    _L1_gnn_all = _L1_gnn_setup()
    _L1_gnn_in = {k: v for k, v in _L1_gnn_all.items() if k in ('gamma', 'beta', 'W_self', 'W_neigh')}
    del _L1_gnn_all

    def _L2_gnn_setup():
        import jax, jax.numpy as jnp
        import numpy as np
        key = jax.random.key(seed)
        k1, k2, k3, k4 = jax.random.split(key, 4)
        B, N, F_in, F_out = (8, 1024, 128, 128)
        inp = jax.random.normal(k1, (B, N, F_in), dtype=jnp.float32)
        adj = jax.random.uniform(k2, (B, N, N), dtype=jnp.float32)
        stdv = 1.0 / np.sqrt(F_out)
        weight = jax.random.uniform(k3, (F_in, F_out), dtype=jnp.float32, minval=-stdv, maxval=stdv)
        bias = jax.random.uniform(k4, (F_out,), dtype=jnp.float32, minval=-stdv, maxval=stdv)
        return {'input': inp, 'adj': adj, 'weight': weight, 'bias': bias}
    _L2_gnn_all = _L2_gnn_setup()
    _L2_gnn_in = {k: v for k, v in _L2_gnn_all.items() if k in ('weight', 'bias')}
    del _L2_gnn_all

    def _L3_gnn_setup():
        import jax, jax.numpy as jnp
        import numpy as np
        from jax import lax
        DIM = 128
        EPS = 1e-05

        def _bn(h, g, b, m, v):
            scale = g / jnp.sqrt(v + EPS)
            return h * scale[None, :, None] + (b - m * scale)[None, :, None]

        def _conv1d(h, w, pad):
            return lax.conv_general_dilated(h, w, window_strides=(1,), padding=[(pad, pad)], dimension_numbers=('NCH', 'OIH', 'NCH'))
        key = jax.random.key(seed)
        ks = jax.random.split(key, 16)
        bs, n, d = (16, 1024, DIM)
        s = 0.05
        return {'x': jax.random.normal(ks[0], (bs, n, d), jnp.float32), 'mask': jnp.ones((bs, n, n), jnp.float32), 'w_se': jax.random.normal(ks[1], (3, d), jnp.float32) * s, 'b_se': jnp.zeros((3,), jnp.float32), 'conv1_w': jax.random.normal(ks[2], (d, d, 1), jnp.float32) * s, 'bn1_g': jnp.ones((d,), jnp.float32), 'bn1_b': jnp.zeros((d,), jnp.float32), 'bn1_m': jnp.zeros((d,), jnp.float32), 'bn1_v': jnp.ones((d,), jnp.float32), 'conv2_w': jax.random.normal(ks[3], (d, d, 17), jnp.float32) * s, 'bn2_g': jnp.ones((d,), jnp.float32), 'bn2_b': jnp.zeros((d,), jnp.float32), 'bn2_m': jnp.zeros((d,), jnp.float32), 'bn2_v': jnp.ones((d,), jnp.float32), 'w_msg': jax.random.normal(ks[4], (d, d), jnp.float32) * s, 'b_msg': jnp.zeros((d,), jnp.float32), 'w_ih': jax.random.normal(ks[5], (3 * d, 2 * d), jnp.float32) * s, 'b_ih': jnp.zeros((3 * d,), jnp.float32), 'w_hh': jax.random.normal(ks[6], (3 * d, d), jnp.float32) * s, 'b_hh': jnp.zeros((3 * d,), jnp.float32)}
    _L3_gnn_all = _L3_gnn_setup()
    _L3_gnn_in = {k: v for k, v in _L3_gnn_all.items() if k in ('w_se', 'b_se', 'conv1_w', 'bn1_g', 'bn1_b', 'bn1_m', 'bn1_v', 'conv2_w', 'bn2_g', 'bn2_b', 'bn2_m', 'bn2_v', 'w_msg', 'b_msg', 'w_ih', 'b_ih', 'w_hh', 'b_hh')}
    del _L3_gnn_all
    return {'x': x, 'adj': adj, 'nodemask': nodemask, 'L0_gnn_W': _L0_gnn_in['W'], 'L0_gnn_b': _L0_gnn_in['b'], 'L1_gnn_gamma': _L1_gnn_in['gamma'], 'L1_gnn_beta': _L1_gnn_in['beta'], 'L1_gnn_W_self': _L1_gnn_in['W_self'], 'L1_gnn_W_neigh': _L1_gnn_in['W_neigh'], 'L2_gnn_weight': _L2_gnn_in['weight'], 'L2_gnn_bias': _L2_gnn_in['bias'], 'L3_gnn_w_se': _L3_gnn_in['w_se'], 'L3_gnn_b_se': _L3_gnn_in['b_se'], 'L3_gnn_conv1_w': _L3_gnn_in['conv1_w'], 'L3_gnn_bn1_g': _L3_gnn_in['bn1_g'], 'L3_gnn_bn1_b': _L3_gnn_in['bn1_b'], 'L3_gnn_bn1_m': _L3_gnn_in['bn1_m'], 'L3_gnn_bn1_v': _L3_gnn_in['bn1_v'], 'L3_gnn_conv2_w': _L3_gnn_in['conv2_w'], 'L3_gnn_bn2_g': _L3_gnn_in['bn2_g'], 'L3_gnn_bn2_b': _L3_gnn_in['bn2_b'], 'L3_gnn_bn2_m': _L3_gnn_in['bn2_m'], 'L3_gnn_bn2_v': _L3_gnn_in['bn2_v'], 'L3_gnn_w_msg': _L3_gnn_in['w_msg'], 'L3_gnn_b_msg': _L3_gnn_in['b_msg'], 'L3_gnn_w_ih': _L3_gnn_in['w_ih'], 'L3_gnn_b_ih': _L3_gnn_in['b_ih'], 'L3_gnn_w_hh': _L3_gnn_in['w_hh'], 'L3_gnn_b_hh': _L3_gnn_in['b_hh']}

def reference(x, adj, nodemask, L0_gnn_W, L0_gnn_b, L1_gnn_gamma, L1_gnn_beta, L1_gnn_W_self, L1_gnn_W_neigh, L2_gnn_weight, L2_gnn_bias, L3_gnn_w_se, L3_gnn_b_se, L3_gnn_conv1_w, L3_gnn_bn1_g, L3_gnn_bn1_b, L3_gnn_bn1_m, L3_gnn_bn1_v, L3_gnn_conv2_w, L3_gnn_bn2_g, L3_gnn_bn2_b, L3_gnn_bn2_m, L3_gnn_bn2_v, L3_gnn_w_msg, L3_gnn_b_msg, L3_gnn_w_ih, L3_gnn_b_ih, L3_gnn_w_hh, L3_gnn_b_hh):
    import jax
    import jax.numpy as jnp

    def _L0_gnn_ref(H, A, mask, W, b):
        import jax, jax.numpy as jnp
        import numpy as np
        EPS = 1e-08
        N = A.shape[-1]
        A_hat = A + jnp.eye(N, dtype=A.dtype)
        deg = A_hat.sum(axis=-1)
        dis = (deg + EPS) ** (-0.5)
        A_norm = dis[:, :, None] * A_hat * dis[:, None, :]
        H_lin = jnp.einsum('bni,oi->bno', H, W) + b
        out = jnp.einsum('bnm,bmo->bno', A_norm, H_lin)
        out = out * mask[:, :, None]
        return jax.nn.relu(out)

    def _L1_gnn_ref(x, adj, gamma, beta, W_self, W_neigh):
        import jax, jax.numpy as jnp
        import numpy as np
        LN_EPS = 1e-05
        mu = jnp.mean(x, axis=-1, keepdims=True)
        var = jnp.mean(jnp.square(x - mu), axis=-1, keepdims=True)
        xn = (x - mu) * jax.lax.rsqrt(var + LN_EPS) * gamma + beta
        d_out = jnp.sum(adj, axis=1)
        d_in = jnp.sum(adj, axis=2)
        s_out = jnp.where(d_out != 0, jax.lax.rsqrt(d_out), 0.0)
        s_in = jnp.where(d_in != 0, jax.lax.rsqrt(d_in), 0.0)
        A_norm = s_out[:, :, None] * adj * s_in[:, None, :]
        eye = jnp.eye(adj.shape[1], dtype=adj.dtype)
        L = eye[None, :, :] - A_norm
        neighbor = jnp.einsum('bij,bjf->bif', L, xn)
        pre = xn @ W_self + neighbor @ W_neigh
        return jax.nn.softplus(pre)

    def _L2_gnn_ref(input, adj, weight, bias):
        import jax, jax.numpy as jnp
        import numpy as np
        d = adj.sum(axis=1) ** (-0.5)
        adj_norm = d[:, :, None] * adj * d[:, None, :]
        support = jnp.einsum('bnf,fo->bno', input, weight)
        output = jnp.einsum('bnm,bmo->bno', adj_norm, support) + bias
        return output

    def _L3_gnn_ref(x, mask, w_se, b_se, conv1_w, bn1_g, bn1_b, bn1_m, bn1_v, conv2_w, bn2_g, bn2_b, bn2_m, bn2_v, w_msg, b_msg, w_ih, b_ih, w_hh, b_hh):
        import jax, jax.numpy as jnp
        import numpy as np
        from jax import lax
        DIM = 128
        EPS = 1e-05

        def _bn(h, g, b, m, v):
            scale = g / jnp.sqrt(v + EPS)
            return h * scale[None, :, None] + (b - m * scale)[None, :, None]

        def _conv1d(h, w, pad):
            return lax.conv_general_dilated(h, w, window_strides=(1,), padding=[(pad, pad)], dimension_numbers=('NCH', 'OIH', 'NCH'))
        d = x.shape[-1]
        xc = jnp.transpose(x, (0, 2, 1))
        h = _bn(_conv1d(xc, conv1_w, 0), bn1_g, bn1_b, bn1_m, bn1_v)
        h = jax.nn.relu(h)
        h = _bn(_conv1d(h, conv2_w, 8), bn2_g, bn2_b, bn2_m, bn2_v)
        x_conv = jnp.transpose(jax.nn.relu(h + xc), (0, 2, 1))
        s = x @ w_se.T + b_se
        sq = jnp.sum(s * s, axis=-1)
        dist = sq[:, :, None] + sq[:, None, :] - 2.0 * jnp.einsum('bnd,bmd->bnm', s, s)
        A = jnp.exp(-dist) * mask
        msg = jax.nn.relu(x @ w_msg.T + b_msg)
        x_nmp = jnp.einsum('bnm,bmd->bnd', A, msg)
        x_in = jnp.concatenate([x_conv, x_nmp], axis=-1)
        gi = x_in @ w_ih.T + b_ih
        gh = x @ w_hh.T + b_hh
        gi_r, gi_z, gi_n = (gi[..., :d], gi[..., d:2 * d], gi[..., 2 * d:])
        gh_r, gh_z, gh_n = (gh[..., :d], gh[..., d:2 * d], gh[..., 2 * d:])
        r = jax.nn.sigmoid(gi_r + gh_r)
        z = jax.nn.sigmoid(gi_z + gh_z)
        nn_ = jnp.tanh(gi_n + r * gh_n)
        return (1.0 - z) * nn_ + z * x
    h = jnp.maximum(_layernorm(x, axis=-1), 0.0)
    x = x + _L0_gnn_ref(h, adj, nodemask, L0_gnn_W, L0_gnn_b)
    h = jnp.maximum(_layernorm(x, axis=-1), 0.0)
    x = x + _L1_gnn_ref(h, adj, L1_gnn_gamma, L1_gnn_beta, L1_gnn_W_self, L1_gnn_W_neigh)
    h = jnp.maximum(_layernorm(x, axis=-1), 0.0)
    x = x + _L2_gnn_ref(h, adj, L2_gnn_weight, L2_gnn_bias)
    h = jnp.maximum(_layernorm(x, axis=-1), 0.0)
    x = x + _L3_gnn_ref(h, adj, L3_gnn_w_se, L3_gnn_b_se, L3_gnn_conv1_w, L3_gnn_bn1_g, L3_gnn_bn1_b, L3_gnn_bn1_m, L3_gnn_bn1_v, L3_gnn_conv2_w, L3_gnn_bn2_g, L3_gnn_bn2_b, L3_gnn_bn2_m, L3_gnn_bn2_v, L3_gnn_w_msg, L3_gnn_b_msg, L3_gnn_w_ih, L3_gnn_b_ih, L3_gnn_w_hh, L3_gnn_b_hh)
    return x

_drawn_inputs = setup_inputs


def setup_inputs(seed=0):
    import zlib

    import numpy as np

    out = dict(_drawn_inputs(seed))
    spreads = {'L0_gnn_b': (0.0, 0.1),
     'L1_gnn_gamma': (1.0, 0.2),
     'L1_gnn_beta': (0.0, 0.1),
     'L3_gnn_b_se': (0.0, 2.0),
     'L3_gnn_bn1_g': (1.0, 0.6),
     'L3_gnn_bn1_b': (0.0, 0.585),
     'L3_gnn_bn1_m': (0.0, 0.492),
     'L3_gnn_bn1_v': (1.0, 0.6),
     'L3_gnn_bn2_g': (1.0, 0.6),
     'L3_gnn_bn2_b': (0.0, 0.8),
     'L3_gnn_bn2_m': (0.0, 0.8),
     'L3_gnn_bn2_v': (1.0, 0.6),
     'L3_gnn_b_msg': (0.0, 1.863),
     'L3_gnn_b_ih': (0.0, 0.408),
     'L3_gnn_b_hh': (0.0, 0.572)}
    factors = {'L3_gnn_w_se': 23.779, 'L3_gnn_w_msg': 3.361}
    for name, (base, spread) in spreads.items():
        noise = np.random.default_rng([zlib.crc32(name.encode()), seed]).standard_normal(out[name].shape)
        drawn = base * np.exp(spread * noise) if base else spread * noise
        out[name] = jnp.asarray(drawn.astype(out[name].dtype))
    for name, factor in factors.items():
        out[name] = (out[name] * factor).astype(out[name].dtype)
    return out
```

```python
import concourse.bass as bass
from concourse import mybir
from contextlib import ExitStack


P = 128
GRAPHS = 128
G = 4
NG = GRAPHS // G
GP = G * P
TAPS = 17
PAD = TAPS // 2
ROW = P + 2 * PAD
LN_EPS = 1e-5
EXP_LN_TABLES = 6
DEG_EPS = 1e-8

W_CONV2, W_CONV1, W_MSG, W_SE, W_IH, W_HH = 0, TAPS, TAPS + 1, TAPS + 2, TAPS + 3, TAPS + 9
NW = TAPS + 12

VECS = ["gamma", "beta", "bn1_g", "bn1_b", "bn1_m", "bn1_v", "bn2_g", "bn2_b", "bn2_m", "bn2_v",
        "b_ih_r", "b_ih_z", "b_ih_n", "b_hh_r", "b_hh_z", "b_hh_n"]


def graph_net(nc, x, adj, mask_t, w0_t, w1_self, w1_neigh, w2, conv2_t, conv1_t, msg_t, se_t, ih_t,
              hh_t, vecs, b_se, rows, out):
    f32, f32r, bf16 = mybir.dt.float32, mybir.dt.float32r, mybir.dt.bfloat16
    ALU = mybir.AluOpType
    ACT = mybir.ActivationFunctionType
    AX = mybir.AxisListType

    x_g = x.rearrange("(s g) n f -> s n g f", g=G)
    adj_g = adj.rearrange("(s g) n m -> s n g m", g=G)
    out_g = out.rearrange("(s g) n f -> s n g f", g=G)

    with ExitStack() as ctx:
        def sb(name, shape, dt=f32):
            return ctx.enter_context(nc.sbuf_tensor(name, shape, dt))

        w_raw = sb("w_raw", [P, NW, P])
        w_hi = sb("w_hi", [P, NW, P], f32r)
        w_lo = sb("w_lo", [P, NW, P], f32r)
        w0 = sb("w0", [P, P])
        w1n = sb("w1n", [P, P])
        w1s = sb("w1s", [P, P])
        w1ns = sb("w1ns", [P, P])
        w2_sb = sb("w2_sb", [P, P])
        ident = sb("ident", [P, P])
        vec = sb("vec", [P, len(VECS)])
        bnp = sb("bnp", [P, 2])
        neg_half = sb("neg_half", [P, 12])
        bns = sb("bns", [P, 2])
        bnr = sb("bnr", [P, 2])
        bnb = sb("bnb", [P, 2])
        gb = sb("gb", [P, 4])
        bse = sb("bse", [P, 1])
        b0_bc = sb("b0_bc", [P, P])
        b2_bc = sb("b2_bc", [P, P])
        bm_f = sb("bm_f", [P, P])
        bm_r = sb("bm_r", [P, P])
        bm3 = sb("bm3", [96, G, P], bf16)
        ones = sb("ones", [96, P], bf16)
        mask_sb = sb("mask_sb", [P, GRAPHS])

        x_in = sb("x_in", [P, 2, G, P])
        adj_in = sb("adj_in", [P, 2, G, P])
        adj_t = sb("adj_t", [P, 2, G, P])
        st0 = sb("st0", [P, G, 6])
        mv0 = sb("mv0", [P, G, 2])
        deg = sb("deg", [P, G])
        deg0 = sb("deg0", [P, G])
        pin0 = sb("pin0", [P, 12])
        rs0 = sb("rs0", [P, 12])
        r0d = sb("r0d", [P, G])
        nm0 = sb("nm0", [P, G])
        dm = sb("dm", [P, G])
        s_in = sb("s_in", [P, G])
        cin = sb("cin", [P, 8])
        cs0 = sb("cs0", [P, G])
        crs = sb("crs", [P, 2, 8])
        ns_out = sb("ns_out", [P, 2, G])
        xh0 = sb("xh0", [P, G, P])
        h0t = sb("h0t", [P, G, P])
        y0 = sb("y0", [P, G, P])
        t0 = sb("t0", [P, G, P])
        u0 = sb("u0", [P, G, P])
        x1 = sb("x1", [P, G, P])

        st1 = sb("st1", [P, G, 6])
        mv1 = sb("mv1", [P, G, 2])
        e1 = sb("e1", [P, G])
        cc = sb("cc", [P, G, P])
        stc = sb("stc", [P, G, 6])
        mvc = sb("mvc", [P, G, 2])
        pin1 = sb("pin1", [P, G])
        q1 = sb("q1", [P, G])
        nmq = sb("nmq", [P, G])
        z1 = sb("z1", [P, G, P])
        z1t = sb("z1t", [P, G, P])
        y1 = sb("y1", [P, G, P])
        self1 = sb("self1", [P, G, P])
        pre = sb("pre", [P, G, P])
        sp_a = sb("sp_a", [P, G, P])
        sp_e = sb("sp_e", [P, G, P])
        sp_l = sb("sp_l", [P, G, P])
        sp = sb("sp", [P, G, P])
        x2 = sb("x2", [P, G, P])
        x2b = sb("x2b", [P, G, P])
        st2 = sb("st2", [P, G, 6])
        mv2 = sb("mv2", [P, G, 2])
        pin2 = sb("pin2", [P, G])
        rs2 = sb("rs2", [P, G])
        r2d = sb("r2d", [P, G])
        xh2 = sb("xh2", [P, G, P])
        h2t = sb("h2t", [P, G, P])
        y2 = sb("y2", [P, G, P])
        x3 = sb("x3", [P, 2, G, P])
        st3 = sb("st3", [P, G, 6])
        mv3 = sb("mv3", [P, G, 2])
        pin3 = sb("pin3", [P, G])
        rs3 = sb("rs3", [P, G])
        xh3 = sb("xh3", [P, G, P])

        ht = sb("ht", [P, 2, G, P])
        ht_hi = sb("ht_hi", [P, 2, G, P], f32r)
        ht_lo = sb("ht_lo", [P, 2, G, P], f32r)
        htb = sb("htb", [P, G, P])
        c1 = sb("c1", [P, G, P])
        c1_hi = sb("c1_hi", [P, G, ROW], f32r)
        c1_lo = sb("c1_lo", [P, G, ROW], f32r)
        msg = sb("msg", [P, G, P])
        dl = sb("dl", [96, G, P])
        dr = sb("dr", [96, G, P])
        ex = sb("ex", [P, G, P])
        m3 = sb("m3", [P, G, P])
        xn_hi = sb("xn_hi", [P, G, P], f32r)
        xn_lo = sb("xn_lo", [P, G, P], f32r)

        cv = sb("cv", [P, G, P])
        xc_hi = sb("xc_hi", [P, G, P], f32r)
        xc_lo = sb("xc_lo", [P, G, P], f32r)
        ge = sb("ge", [P, 2, GP])
        gl = sb("gl", [P, 2, GP])
        rz = sb("rz", [P, 2, GP])
        rn = sb("rn", [P, GP])
        vn = sb("vn", [P, GP])
        ne = sb("ne", [P, GP])
        nl = sb("nl", [P, GP])
        nq = sb("nq", [P, GP])
        nn = sb("nn", [P, GP])
        hd = sb("hd", [P, GP])
        zd = sb("zd", [P, GP])
        ot = sb("ot", [P, G, P])
        x4 = sb("x4", [P, 2, G, P])

        def bank(name):
            return ctx.enter_context(nc.psum_tensor(name, [P, G, P], f32))

        CB = bank("bank_conv")
        GR, GZ, GI, GH = bank("bank_r"), bank("bank_z"), bank("bank_in"), bank("bank_hn")
        XA, XB, XC = bank("bank_a"), bank("bank_b"), bank("bank_c")

        def flat(t):
            return t.rearrange("p g n -> p (g n)")

        names = """
            loads_weights loads_consts ident_zero ident_made halves_set bn_in bn_pow bn_scale bn_shift
            weights_hi weights_split se_zero gate_bias pads_set bm_hi bm_r1 bm_mid bm_r2 bm3_made w1_sum
            x_loaded_0 x_loaded_1 adj_loaded_0 adj_loaded_1 x_stored_0 x_stored_1
            st0_done mv0_done deg_done deg0_done pin0_done rs0_done r0d_done nm0_done dm_done xh0_done
            adj_t_psum adj_t_done h0t_psum h0t_done cs0_done is0_done cin_done crs_done ns_done
            w0_done y0_done a0_done t0_done u0_done x1_done
            st1_done mv1_done e1_done c_done stc_done mvc_done pin1_done q1_done nmq_done z1_done
            z1t_psum z1t_done w1_done y1_done self1_done a1_done pre_done spa_done spe_done spl_done
            sp_done x2_done x2b_done st2_done mv2_done pin2_done rs2_done r2d_done xh2_done
            h2t_psum h2t_done w2_done y2_done a2_done x3_done st3_done mv3_done pin3_done rs3_done
            xh3_done
            ht_psum ht_done ht_hi_done ht_lo_done htb_done conv1_done c1_done c1_hi_done c1_lo_done
            se_done dl_s dr_s dl_q dr_q msg_psum msg_done dist_done ex_done m3_done
            a3_done xn_hi_done xn_lo_done conv2_done
            cv_done xc_hi_done xc_lo_done gate_h_done gates_done ge_done gl_done rz_done rn_done vn_done
            ne_done nl_done nq_done nn_done hd_done zd_done ot_done ot_psum x4_done
            tick_dve tick_sp
        """.split()
        S = {n: ctx.enter_context(nc.semaphore(n)) for n in names}

        x_loaded, adj_loaded = (S["x_loaded_0"], S["x_loaded_1"]), (S["adj_loaded_0"], S["adj_loaded_1"])
        x_stored = (S["x_stored_0"], S["x_stored_1"])

        def wait(eng, sem, n):
            if not isinstance(n, int) or n > 0:
                eng.wait_ge(sem, n)

        def steps(eng, body):
            def peeled(k):
                body(k, k // 2, k % 2, 0 <= k + 2 < NG, 0 <= k + 1 < NG, 0 <= k < NG, 0 <= k - 1 < NG)

            for k in range(-2, 4):
                peeled(k)
            with eng.Fori(2, (NG - 2) // 2) as j:
                for p in range(2):
                    body(j * 2 + p, j, p, True, True, True, True)
            for k in range(NG - 2, NG + 1):
                peeled(k)

        block = ctx.enter_context(nc.Block())

        @block.sync
        def _(sp):
            n_w = 0
            for dst, src in ((w0[:], w0_t), (w1n[:], w1_neigh), (w1s[:], w1_self), (w2_sb[:], w2),
                             (vec[:], vecs), (mask_sb[:], mask_t),
                             (b0_bc[:], rows[0:1, :].broadcast_to([P, P])),
                             (b2_bc[:], rows[1:2, :].broadcast_to([P, P])),
                             (bm_f[:], rows[2:3, :].broadcast_to([P, P]))):
                sp.dma_start(dst, src).then_inc(S["loads_consts"], 16)
                n_w += 1
            assert n_w == 9

            def load(g, slot):
                wait(sp, S["x1_done"], g - 1)
                sp.sem_inc(S["tick_sp"], 1)
                sp.dma_start(x_in[:, slot], x_g[g]).then_inc(x_loaded[slot], 16)
                wait(sp, S["deg_done"], g - 1)
                sp.sem_inc(S["tick_sp"], 1)
                wait(sp, S["adj_t_psum"], g - 1)
                sp.sem_inc(S["tick_sp"], 1)
                sp.dma_start(adj_in[:, slot], adj_g[g]).then_inc(adj_loaded[slot], 16)

            def load_weights():
                sp.wait_ge(S["se_zero"], 2)
                sp.dma_start(w_raw[:, W_CONV2:W_CONV2 + TAPS, :], conv2_t).then_inc(S["loads_weights"], 16)
                sp.dma_start(w_raw[:, W_CONV1, :], conv1_t).then_inc(S["loads_weights"], 16)
                sp.dma_start(w_raw[:, W_MSG, :], msg_t).then_inc(S["loads_weights"], 16)
                sp.dma_start(w_raw[:, W_IH:W_IH + 6, :], ih_t).then_inc(S["loads_weights"], 16)
                sp.dma_start(w_raw[:, W_HH:W_HH + 3, :], hh_t).then_inc(S["loads_weights"], 16)
                for r in range(3):
                    sp.dma_start(w_raw[:, W_SE, 32 * r:32 * r + 3], se_t).then_inc(S["loads_weights"], 16)
                    sp.dma_start(bse[32 * r:32 * r + 3, 0:1], b_se).then_inc(S["loads_weights"], 16)

            def body(k, u, p, gcn, mid, conv, gate):
                if gcn:
                    load(k + 2, p)
                if isinstance(k, int) and k == -1:
                    load_weights()
                if gate:
                    wait(sp, S["x4_done"], k)
                    sp.sem_inc(S["tick_sp"], 1)
                    sp.dma_start(out_g[k - 1], x4[:, (p + 1) % 2]).then_inc(x_stored[(p + 1) % 2], 16)

            steps(sp, body)
            sp.wait_ge(S["x_stored_0"], 16 * NG // 2)
            sp.wait_ge(S["x_stored_1"], 16 * NG // 2)

        @block.gpsimd
        def _(pool):
            nc.gpsimd.memset(w_raw[:, W_SE, :], 0.0).then_inc(S["se_zero"], 1)
            nc.gpsimd.memset(bse[:], 0.0).then_inc(S["se_zero"], 1)
            nc.gpsimd.memset(neg_half[:], -0.5).then_inc(S["halves_set"], 1)
            nc.gpsimd.memset(ident[:], 0.0).then_inc(S["ident_zero"], 1)
            pool.wait_ge(S["ident_zero"], 1)
            nc.gpsimd.affine_select(out=ident[:], in_=ident[:], compare_op=ALU.not_equal, fill=1.0, base=0,
                                    pattern=[[-1, P]], channel_multiplier=1).then_inc(S["ident_made"], 1)
            pool.wait_ge(S["halves_set"], 1)
            pool.wait_ge(S["bn_in"], 1)
            nc.gpsimd.tensor_tensor(bnr[:], bnp[:], neg_half[:, 0:2], ALU.pow).then_inc(S["bn_pow"], 1)
            nc.gpsimd.memset(c1_hi[:].bitcast(f32), 0.0).then_inc(S["pads_set"], 1)
            nc.gpsimd.memset(c1_lo[:].bitcast(f32), 0.0).then_inc(S["pads_set"], 1)

            def body(k, u, p, gcn, mid, conv, gate):
                q = (p + 1) % 2
                if conv:
                    wait(pool, S["ht_done"], k + 1)
                    wait(pool, S["bn_shift"], 1)
                    wait(pool, S["cv_done"], k)
                    nc.gpsimd.tensor_tensor(htb[:], ht[:, p], bnb[:, 1:2].unsqueeze(2).broadcast_to([P, G, P]),
                                            ALU.add).then_inc(S["htb_done"], 1)
                if mid:
                    wait(pool, S["pin1_done"], k + 2)
                    wait(pool, S["z1_done"], k + 1)
                    nc.gpsimd.tensor_tensor(q1[:], pin1[:], neg_half[:, 0:G], ALU.pow).then_inc(S["q1_done"], 1)
                if gcn:
                    wait(pool, S["pin0_done"], k + 3)
                    wait(pool, S["dm_done"], k + 2)
                    wait(pool, S["y0_done"], k + 2)
                    nc.gpsimd.tensor_tensor(rs0[:], pin0[:], neg_half[:, 0:12], ALU.pow).then_inc(S["rs0_done"], 1)
                if gate:
                    wait(pool, S["nn_done"], k)
                    wait(pool, S["ht_done"], k)
                    nc.gpsimd.tensor_tensor(hd[:], flat(ht[:, q]), nn[:], ALU.subtract).then_inc(S["hd_done"], 1)
                    wait(pool, S["rz_done"], k)
                    wait(pool, S["hd_done"], k)
                    nc.gpsimd.tensor_tensor(zd[:], hd[:], rz[:, 1], ALU.mult).then_inc(S["zd_done"], 1)
                    wait(pool, S["zd_done"], k)
                    wait(pool, S["ot_psum"], k - 1)
                    nc.gpsimd.tensor_tensor(flat(ot[:]), zd[:], nn[:], ALU.add).then_inc(S["ot_done"], 1)
                if conv:
                    wait(pool, S["ex_done"], k + 1)
                    wait(pool, S["adj_t_done"], k + 1)
                    wait(pool, S["a3_done"], k)
                    nc.gpsimd.tensor_tensor(m3[:], ex[:], adj_t[:, p], ALU.mult).then_inc(S["m3_done"], 1)
                if mid:
                    wait(pool, S["pin2_done"], k + 2)
                    nc.gpsimd.tensor_tensor(rs2[:], pin2[:], neg_half[:, 0:G], ALU.pow).then_inc(S["rs2_done"], 1)
                if gcn:
                    wait(pool, S["cin_done"], k + 3)
                    wait(pool, S["x3_done"], k + 1)
                    nc.gpsimd.tensor_tensor(crs[:, p], cin[:], neg_half[:, 0:8], ALU.pow).then_inc(S["crs_done"], 1)
                if mid:
                    wait(pool, S["loads_consts"], 9 * 16)
                    wait(pool, S["x2_done"], k + 2)
                    wait(pool, S["x3_done"], k + 1)
                    nc.gpsimd.tensor_tensor(x2b[:], x2[:], b2_bc[:].unsqueeze(1).broadcast_to([P, G, P]),
                                            ALU.add).then_inc(S["x2b_done"], 1)
                if gcn:
                    wait(pool, S["u0_done"], k + 3)
                    wait(pool, x_loaded[p], (u + 2) * 16)
                    wait(pool, S["x2_done"], k + 2)
                    wait(pool, S["c_done"], k + 2)
                    nc.gpsimd.tensor_tensor(x1[:], x_in[:, p], u0[:], ALU.add).then_inc(S["x1_done"], 1)
                if mid:
                    wait(pool, S["pin3_done"], k + 2)
                    wait(pool, S["xh3_done"], k + 1)
                    nc.gpsimd.tensor_tensor(rs3[:], pin3[:], neg_half[:, 0:G], ALU.pow).then_inc(S["rs3_done"], 1)

            steps(pool, body)

        @block.scalar
        def _(act):
            nc.scalar.add_instruction(mybir.InstLoadActFuncSet(
                name=nc.get_next_instruction_name(), engine=mybir.EngineType.Activation, act_func_set_id=EXP_LN_TABLES))

            def scaled(dst, src, scale, shift, sem):
                for g in range(G):
                    last = nc.scalar.activation(dst[:, g], src[:, g], ACT.Identity, bias=shift[:, g:g + 1],
                                                scale=scale[:, g:g + 1])
                last.then_inc(sem, 1)

            def body(k, u, p, gcn, mid, conv, gate):
                if gate:
                    act.wait_ge(S["cv_done"], k)
                    wait(act, S["gates_done"], k - 1)
                    nc.scalar.activation(xc_hi[:], cv[:], ACT.Relu).then_inc(S["xc_hi_done"], 1)
                if conv:
                    act.wait_ge(S["ht_psum"], k + 1)
                    wait(act, S["hd_done"], k - 1)
                    wait(act, S["htb_done"], k)
                    nc.scalar.activation(ht[:, p], XA[:], ACT.Relu).then_inc(S["ht_done"], 1)
                    wait(act, S["gate_h_done"], k - 1)
                    nc.scalar.activation(ht_hi[:, p], XA[:], ACT.Relu).then_inc(S["ht_hi_done"], 1)
                if gate:
                    act.wait_ge(S["gates_done"], k)
                    act.wait_ge(S["gate_bias"], 3)
                    wait(act, S["gl_done"], k - 1)
                    nc.scalar.activation(ge[:, 0], flat(GR[:]), ACT.Exp, bias=gb[:, 0:1], scale=-1.0)
                    nc.scalar.activation(ge[:, 1], flat(GZ[:]), ACT.Exp, bias=gb[:, 1:2],
                                         scale=-1.0).then_inc(S["ge_done"], 1)
                if conv:
                    act.wait_ge(S["conv1_done"], k + 1)
                    act.wait_ge(S["bn_shift"], 1)
                    wait(act, S["c1_lo_done"], k)
                    nc.scalar.activation(c1[:], CB[:], ACT.Relu, bias=bnb[:, 0:1],
                                         scale=bns[:, 0:1]).then_inc(S["c1_done"], 1)
                    act.wait_ge(S["pads_set"], 5)
                    wait(act, S["conv2_done"], k)
                    nc.scalar.activation(c1_hi[:, :, PAD:PAD + P], CB[:], ACT.Relu, bias=bnb[:, 0:1],
                                         scale=bns[:, 0:1]).then_inc(S["c1_hi_done"], 1)
                if mid:
                    act.wait_ge(S["nmq_done"], k + 2)
                    act.wait_ge(S["q1_done"], k + 2)
                    wait(act, S["z1t_psum"], k + 1)
                    scaled(z1, cc, q1, nmq, S["z1_done"])
                if gate:
                    act.wait_ge(S["ge_done"], k)
                    nc.scalar.activation(gl[:], ge[:], ACT.Ln, bias=1.0).then_inc(S["gl_done"], 1)
                if conv:
                    act.wait_ge(S["se_done"], k + 1)
                    act.wait_ge(S["loads_weights"], 11 * 16)
                    wait(act, S["dist_done"], k)
                    nc.scalar.activation(dl[32:64], XB[32:64], ACT.Square, bias=bse[32:64, 0:1]).then_inc(S["dl_q"], 1)
                    nc.scalar.activation(dr[64:96], XB[64:96], ACT.Square, bias=bse[64:96, 0:1]).then_inc(S["dr_q"], 1)
                    nc.scalar.activation(dl[0:32], XB[0:32], ACT.Identity, bias=bse[0:32, 0:1]).then_inc(S["dl_s"], 1)
                if mid:
                    act.wait_ge(S["z1t_psum"], k + 2)
                    act.wait_ge(S["loads_consts"], 9 * 16)
                    wait(act, S["w1_done"], k + 1)
                    nc.scalar.activation(z1t[:], XC[:], ACT.Identity, bias=vec[:, 1:2],
                                         scale=vec[:, 0:1]).then_inc(S["z1t_done"], 1)
                if gate:
                    act.wait_ge(S["gl_done"], k)
                    wait(act, S["rn_done"], k - 1)
                    wait(act, S["zd_done"], k - 1)
                    nc.scalar.activation(rz[:], gl[:], ACT.Exp, scale=-1.0).then_inc(S["rz_done"], 1)
                if conv:
                    act.wait_ge(S["msg_psum"], k + 1)
                    wait(act, S["a3_done"], k)
                    nc.scalar.activation(msg[:], GR[:], ACT.Relu).then_inc(S["msg_done"], 1)
                if mid:
                    act.wait_ge(S["w1_done"], k + 2)
                    wait(act, S["pre_done"], k + 1)
                    nc.scalar.activation(self1[:], XA[:], ACT.Copy).then_inc(S["self1_done"], 1)
                if gate:
                    act.wait_ge(S["vn_done"], k)
                    wait(act, S["nl_done"], k - 1)
                    nc.scalar.activation(ne[:], vn[:], ACT.Exp, bias=gb[:, 3:4], scale=-2.0).then_inc(S["ne_done"], 1)
                if gcn:
                    act.wait_ge(S["nm0_done"], k + 3)
                    act.wait_ge(x_loaded[p], (u + 2) * 16)
                    wait(act, S["h0t_psum"], k + 2)
                    scaled(xh0, x_in[:, p], r0d, nm0, S["xh0_done"])
                if gate:
                    act.wait_ge(S["ne_done"], k)
                    nc.scalar.activation(nl[:], ne[:], ACT.Ln, bias=1.0).then_inc(S["nl_done"], 1)
                    act.wait_ge(S["nl_done"], k)
                    wait(act, S["nn_done"], k - 1)
                    nc.scalar.activation(nq[:], nl[:], ACT.Exp, scale=-1.0).then_inc(S["nq_done"], 1)
                if mid:
                    act.wait_ge(S["pre_done"], k + 2)
                    nc.scalar.activation(sp_a[:], pre[:], ACT.Abs).then_inc(S["spa_done"], 1)
                    act.wait_ge(S["spa_done"], k + 2)
                    nc.scalar.activation(sp_e[:], sp_a[:], ACT.Exp, scale=-1.0).then_inc(S["spe_done"], 1)
                    act.wait_ge(S["spe_done"], k + 2)
                    wait(act, S["sp_done"], k + 1)
                    nc.scalar.activation(sp_l[:], sp_e[:], ACT.Ln, bias=1.0).then_inc(S["spl_done"], 1)
                if conv:
                    act.wait_ge(S["dist_done"], k + 1)
                    wait(act, S["m3_done"], k)
                    nc.scalar.activation(ex[:], XB[:], ACT.Exp).then_inc(S["ex_done"], 1)
                if gcn:
                    act.wait_ge(S["h0t_psum"], k + 3)
                    wait(act, S["w0_done"], k + 2)
                    nc.scalar.activation(h0t[:], XC[:], ACT.Relu).then_inc(S["h0t_done"], 1)
                    act.wait_ge(S["adj_t_psum"], k + 3)
                    wait(act, S["m3_done"], k + 1)
                    wait(act, S["crs_done"], k + 2)
                    for g in range(G):
                        last = nc.scalar.activation(adj_t[:, p, g], XA[:, g], ACT.Copy, accum_out=cin[:, g:g + 1])
                    last.then_inc(S["adj_t_done"], 1)
                if conv:
                    act.wait_ge(S["a3_done"], k + 1)
                    wait(act, S["gates_done"], k)
                    nc.scalar.activation(xn_hi[:], GI[:], ACT.Copy).then_inc(S["xn_hi_done"], 1)
                if mid:
                    act.wait_ge(S["h2t_psum"], k + 2)
                    wait(act, S["w2_done"], k + 1)
                    nc.scalar.activation(h2t[:], GH[:], ACT.Relu).then_inc(S["h2t_done"], 1)
                if gcn:
                    act.wait_ge(S["t0_done"], k + 3)
                    act.wait_ge(S["dm_done"], k + 3)
                    wait(act, S["x1_done"], k + 2)
                    for g in range(G):
                        last = nc.scalar.activation(u0[:, g], t0[:, g], ACT.Relu, scale=dm[:, g:g + 1])
                    last.then_inc(S["u0_done"], 1)
                if mid:
                    act.wait_ge(S["w2_done"], k + 2)
                    wait(act, S["a2_done"], k + 1)
                    nc.scalar.activation(y2[:], GR[:], ACT.Copy).then_inc(S["y2_done"], 1)

            steps(act, body)

        @block.vector
        def _(dve):
            nc.vector.memset(dl[64:96], -1.0).then_inc(S["pads_set"], 1)
            nc.vector.memset(dr[32:64], -1.0).then_inc(S["pads_set"], 1)
            nc.vector.memset(ones[:], 1.0 / 32).then_inc(S["pads_set"], 1)
            dve.wait_ge(S["loads_consts"], 9 * 16)
            nc.vector.tensor_tensor(w1ns[:], w1s[:], w1n[:], ALU.add).then_inc(S["w1_sum"], 1)
            for i in range(2):
                last = nc.vector.tensor_scalar(bnp[:, i:i + 1], vec[:, 5 + 4 * i:6 + 4 * i], LN_EPS, None, ALU.add)
            last.then_inc(S["bn_in"], 1)
            nc.vector.tensor_copy(bm3[:, 0], bm_f[0:96]).then_inc(S["bm_hi"], 1)
            dve.wait_ge(S["bm_hi"], 1)
            nc.vector.tensor_tensor(bm_r[0:96], bm_f[0:96], bm3[:, 0], ALU.subtract).then_inc(S["bm_r1"], 1)
            dve.wait_ge(S["bm_r1"], 1)
            nc.vector.tensor_copy(bm3[32:64, 0], bm_r[32:64])
            nc.vector.tensor_copy(bm3[64:96, 0], bm_r[64:96]).then_inc(S["bm_mid"], 1)
            dve.wait_ge(S["bm_mid"], 1)
            nc.vector.tensor_tensor(bm_f[64:96], bm_r[64:96], bm3[64:96, 0], ALU.subtract).then_inc(S["bm_r2"], 1)
            dve.wait_ge(S["bm_r2"], 1)
            nc.vector.tensor_copy(bm3[64:96, 0], bm_f[64:96]).then_inc(S["bm_mid"], 1)
            dve.wait_ge(S["bm_mid"], 2)
            for g in range(1, G):
                last = nc.vector.tensor_copy(bm3[:, g], bm3[:, 0])
            last.then_inc(S["bm3_made"], 1)
            nc.vector.tensor_tensor(gb[:, 0:2], vec[:, 10:12], vec[:, 13:15], ALU.add).then_inc(S["gate_bias"], 1)
            dve.wait_ge(S["gate_bias"], 1)
            nc.vector.tensor_scalar(gb[:, 0:2], gb[:, 0:2], -1.0, None, ALU.mult).then_inc(S["gate_bias"], 1)
            nc.vector.tensor_scalar(gb[:, 3:4], vec[:, 12:13], -2.0, None, ALU.mult).then_inc(S["gate_bias"], 1)
            dve.wait_ge(S["bn_pow"], 1)
            for i in range(2):
                last = nc.vector.tensor_tensor(bns[:, i:i + 1], bnr[:, i:i + 1], vec[:, 2 + 4 * i:3 + 4 * i], ALU.mult)
            last.then_inc(S["bn_scale"], 1)
            dve.wait_ge(S["bn_scale"], 1)
            for i in range(2):
                last = nc.vector.tensor_tensor(bnr[:, i:i + 1], bns[:, i:i + 1], vec[:, 4 + 4 * i:5 + 4 * i], ALU.mult)
            last.then_inc(S["bn_scale"], 1)
            dve.wait_ge(S["bn_scale"], 2)
            for i in range(2):
                last = nc.vector.tensor_tensor(bnb[:, i:i + 1], vec[:, 3 + 4 * i:4 + 4 * i], bnr[:, i:i + 1], ALU.subtract)
            last.then_inc(S["bn_shift"], 1)

            def split_weights():
                dve.wait_ge(S["loads_weights"], 11 * 16)
                nc.vector.tensor_copy(w_hi[:], w_raw[:]).then_inc(S["weights_hi"], 1)
                dve.wait_ge(S["weights_hi"], 1)
                nc.vector.tensor_tensor(w_lo[:], w_raw[:], w_hi[:].bitcast(f32), ALU.subtract).then_inc(S["weights_split"], 1)

            def stats(src, st, mv, st_sem, mv_sem, n):
                for g in range(G):
                    last = nc.vector.bn_stats(st[:, g], src[:, g])
                last.then_inc(st_sem, 1)
                dve.wait_ge(st_sem, n)
                dve.sem_inc(S["tick_dve"], 1)
                for g in range(G):
                    last = nc.vector.bn_aggr(mv[:, g], st[:, g])
                last.then_inc(mv_sem, 1)
                dve.wait_ge(mv_sem, n)

            def normalise(dst, src, mv, scale, sem):
                for g in range(G):
                    last = nc.vector.tensor_scalar(dst[:, g], src[:, g], mv[:, g, 0:1], scale[:, g:g + 1],
                                                   ALU.subtract, ALU.mult)
                last.then_inc(sem, 1)

            def body(k, u, p, gcn, mid, conv, gate):
                q = (p + 1) % 2
                if isinstance(k, int) and k == -1:
                    split_weights()
                if gate:
                    dve.wait_ge(S["conv2_done"], k)
                    dve.wait_ge(S["htb_done"], k)
                    nc.vector.scalar_tensor_tensor(cv[:], CB[:], bns[:, 1:2], htb[:], ALU.mult,
                                                   ALU.add).then_inc(S["cv_done"], 1)
                if mid:
                    dve.wait_ge(S["x1_done"], k + 2)
                    stats(x1, st1, mv1, S["st1_done"], S["mv1_done"], k + 2)
                if conv:
                    dve.wait_ge(S["rs3_done"], k + 1)
                    wait(dve, S["ht_psum"], k)
                    normalise(xh3, x3[:, p], mv3, rs3, S["xh3_done"])
                if gate:
                    dve.wait_ge(S["xc_hi_done"], k)
                    nc.vector.scalar_tensor_tensor(xc_lo[:], cv[:], 0.0, xc_hi[:].bitcast(f32), ALU.max,
                                                   ALU.subtract).then_inc(S["xc_lo_done"], 1)
                if mid:
                    nc.vector.tensor_scalar(e1[:], mv1[:, :, 1], LN_EPS, LN_EPS, ALU.add, ALU.mult).then_inc(S["e1_done"], 1)
                    for g in range(G):
                        last = nc.vector.tensor_scalar(cc[:, g], x1[:, g], mv1[:, g, 0:1], mv1[:, g, 0:1],
                                                       ALU.max, ALU.subtract)
                    last.then_inc(S["c_done"], 1)
                    dve.wait_ge(S["c_done"], k + 2)
                    stats(cc, stc, mvc, S["stc_done"], S["mvc_done"], k + 2)
                    nc.vector.tensor_tensor(pin1[:], mvc[:, :, 1], e1[:], ALU.add).then_inc(S["pin1_done"], 1)
                if conv:
                    dve.wait_ge(S["ht_hi_done"], k + 1)
                    wait(dve, S["gate_h_done"], k - 1)
                    nc.vector.tensor_tensor(ht_lo[:, p], ht[:, p], ht_hi[:, p].bitcast(f32),
                                            ALU.subtract).then_inc(S["ht_lo_done"], 1)
                if mid:
                    dve.wait_ge(S["q1_done"], k + 2)
                    nc.vector.scalar_tensor_tensor(nmq[:], mvc[:, :, 0], -1.0, q1[:], ALU.mult,
                                                   ALU.mult).then_inc(S["nmq_done"], 1)
                if conv:
                    dve.wait_ge(S["c1_hi_done"], k + 1)
                    nc.vector.tensor_tensor(c1_lo[:, :, PAD:PAD + P], c1[:], c1_hi[:, :, PAD:PAD + P].bitcast(f32),
                                            ALU.subtract).then_inc(S["c1_lo_done"], 1)
                    dve.wait_ge(S["dl_s"], k + 1)
                    wait(dve, S["dist_done"], k)
                    nc.vector.tensor_scalar(dr[0:32], dl[0:32], 2.0, None, ALU.mult).then_inc(S["dr_s"], 1)
                if gcn:
                    dve.wait_ge(adj_loaded[p], (u + 2) * 16)
                    nc.vector.tensor_reduce(deg[:], adj_in[:, p], AX.X, ALU.add).then_inc(S["deg_done"], 1)
                    dve.wait_ge(S["deg_done"], k + 3)
                    nc.vector.tensor_scalar(deg0[:], deg[:], 0.0, None, ALU.is_equal).then_inc(S["deg0_done"], 1)
                    nc.vector.tensor_scalar(pin0[:, 4:8], deg[:], 1.0, DEG_EPS, ALU.add, ALU.add)
                    dve.wait_ge(x_loaded[p], (u + 2) * 16)
                    stats(x_in[:, p], st0, mv0, S["st0_done"], S["mv0_done"], k + 3)
                    nc.vector.tensor_scalar(pin0[:, 0:4], mv0[:, :, 1], LN_EPS, None, ALU.add)
                    dve.wait_ge(S["deg0_done"], k + 3)
                    nc.vector.tensor_tensor(pin0[:, 8:12], deg[:], deg0[:], ALU.add).then_inc(S["pin0_done"], 1)
                if gate:
                    dve.wait_ge(S["rz_done"], k)
                    nc.vector.scalar_tensor_tensor(rn[:], flat(GH[:]), vec[:, 15:16], rz[:, 0], ALU.add,
                                                   ALU.mult).then_inc(S["rn_done"], 1)
                    dve.wait_ge(S["rn_done"], k)
                    wait(dve, S["ne_done"], k - 1)
                    nc.vector.tensor_tensor(vn[:], flat(GI[:]), rn[:], ALU.add).then_inc(S["vn_done"], 1)
                if mid:
                    dve.wait_ge(S["w1_done"], k + 2)
                    wait(dve, S["a1_done"], k + 1)
                    nc.vector.tensor_tensor(y1[:], XC[:], s_in[:].unsqueeze(2).broadcast_to([P, G, P]),
                                            ALU.mult).then_inc(S["y1_done"], 1)
                if gcn:
                    dve.wait_ge(S["rs0_done"], k + 3)
                    nc.vector.tensor_tensor(r0d[:], rs0[:, 0:4], rs0[:, 4:8], ALU.mult).then_inc(S["r0d_done"], 1)
                    nc.vector.tensor_scalar(deg0[:], deg0[:], -1.0, 1.0, ALU.mult, ALU.add).then_inc(S["is0_done"], 1)
                    mask_cols = mask_sb[:, bass.ds((k + 2) * G, G)] if not isinstance(k, int) else \
                        mask_sb[:, (k + 2) * G:(k + 3) * G]
                    wait(dve, S["u0_done"], k + 2)
                    nc.vector.tensor_tensor(dm[:], rs0[:, 4:8], mask_cols, ALU.mult).then_inc(S["dm_done"], 1)
                    dve.wait_ge(S["r0d_done"], k + 3)
                    nc.vector.scalar_tensor_tensor(nm0[:], mv0[:, :, 0], -1.0, r0d[:], ALU.mult,
                                                   ALU.mult).then_inc(S["nm0_done"], 1)
                    dve.wait_ge(S["is0_done"], k + 3)
                    if mid:
                        dve.wait_ge(S["y1_done"], k + 2)
                    nc.vector.tensor_tensor(s_in[:], rs0[:, 8:12], deg0[:], ALU.mult)
                if gate:
                    dve.wait_ge(S["nq_done"], k)
                    wait(dve, S["ot_done"], k - 1)
                    nc.vector.tensor_scalar(nn[:], nq[:], 2.0, -1.0, ALU.mult, ALU.add).then_inc(S["nn_done"], 1)
                if mid:
                    dve.wait_ge(S["a1_done"], k + 2)
                    dve.wait_ge(S["self1_done"], k + 2)
                    dve.wait_ge(S["ns_done"], k + 2)
                    for g in range(G):
                        last = nc.vector.scalar_tensor_tensor(pre[:, g], GZ[:, g], ns_out[:, q, g:g + 1], self1[:, g],
                                                              ALU.mult, ALU.add)
                    last.then_inc(S["pre_done"], 1)
                    dve.wait_ge(S["spl_done"], k + 2)
                    nc.vector.scalar_tensor_tensor(sp[:], pre[:], 0.0, sp_l[:], ALU.max, ALU.add).then_inc(S["sp_done"], 1)
                    dve.wait_ge(S["sp_done"], k + 2)
                    wait(dve, S["x2b_done"], k + 1)
                    nc.vector.tensor_tensor(x2[:], x1[:], sp[:], ALU.add).then_inc(S["x2_done"], 1)
                    dve.wait_ge(S["x2_done"], k + 2)
                    stats(x2, st2, mv2, S["st2_done"], S["mv2_done"], k + 2)
                    nc.vector.tensor_scalar(pin2[:], mv2[:, :, 1], LN_EPS, None, ALU.add).then_inc(S["pin2_done"], 1)
                if gcn:
                    dve.wait_ge(S["adj_t_done"], k + 3)
                    nc.vector.tensor_scalar(cs0[:], cin[:, 0:4], 0.0, None, ALU.is_equal).then_inc(S["cs0_done"], 1)
                    dve.wait_ge(S["cs0_done"], k + 3)
                    wait(dve, S["crs_done"], k + 2)
                    nc.vector.tensor_tensor(cin[:, 4:8], cin[:, 0:4], cs0[:], ALU.add).then_inc(S["cin_done"], 1)
                if mid:
                    dve.wait_ge(S["rs2_done"], k + 2)
                    nc.vector.tensor_tensor(r2d[:], rs2[:], crs[:, q, 0:4], ALU.mult).then_inc(S["r2d_done"], 1)
                    dve.wait_ge(S["r2d_done"], k + 2)
                    wait(dve, S["h2t_psum"], k + 1)
                    normalise(xh2, x2, mv2, r2d, S["xh2_done"])
                if conv:
                    dve.wait_ge(S["xn_hi_done"], k + 1)
                    nc.vector.tensor_tensor(xn_lo[:], GI[:], xn_hi[:].bitcast(f32), ALU.subtract).then_inc(S["xn_lo_done"], 1)
                if gcn:
                    dve.wait_ge(S["w0_done"], k + 3)
                    wait(dve, S["a0_done"], k + 2)
                    for g in range(G):
                        last = nc.vector.scalar_tensor_tensor(y0[:, g], b0_bc[:], rs0[:, 4 + g:5 + g], GZ[:, g],
                                                              ALU.mult, ALU.add)
                    last.then_inc(S["y0_done"], 1)
                    dve.wait_ge(S["crs_done"], k + 3)
                    nc.vector.scalar_tensor_tensor(ns_out[:, p], cs0[:], -1.0, crs[:, p, 4:8], ALU.add,
                                                   ALU.mult).then_inc(S["ns_done"], 1)
                if gate:
                    dve.wait_ge(S["ot_psum"], k)
                    wait(dve, x_stored[q], (u - 1 + p) * 16)
                    nc.vector.tensor_tensor(x4[:, q], XB[:], x3[:, q], ALU.add).then_inc(S["x4_done"], 1)
                if gcn:
                    dve.wait_ge(S["a0_done"], k + 3)
                    wait(dve, S["u0_done"], k + 2)
                    nc.vector.tensor_tensor(t0[:], GI[:], y0[:], ALU.add).then_inc(S["t0_done"], 1)
                if mid:
                    dve.wait_ge(S["a2_done"], k + 2)
                    dve.wait_ge(S["x2b_done"], k + 2)
                    wait(dve, S["x4_done"], k)
                    for g in range(G):
                        last = nc.vector.scalar_tensor_tensor(x3[:, q, g], GH[:, g], crs[:, q, g:g + 1], x2b[:, g],
                                                              ALU.mult, ALU.add)
                    last.then_inc(S["x3_done"], 1)
                    dve.wait_ge(S["x3_done"], k + 2)
                    stats(x3[:, q], st3, mv3, S["st3_done"], S["mv3_done"], k + 2)
                    nc.vector.tensor_scalar(pin3[:], mv3[:, :, 1], LN_EPS, None, ALU.add).then_inc(S["pin3_done"], 1)

            steps(dve, body)

        @block.tensor
        def _(pe):
            def transposes(dst, src):
                for g in range(G):
                    last = nc.tensor.transpose(dst[:, g], src[:, g], ident[:])
                return last

            def per_graph(dst, lhs, rhs):
                for g in range(G):
                    last = nc.tensor.matmul(dst[:, g], lhs(g), rhs(g), start=True, stop=True)
                return last

            def split_product(dst, w, hi, lo, start, stop):
                nc.tensor.matmul(dst, w_hi[:, w], hi, start=start, stop=False)
                nc.tensor.matmul(dst, w_hi[:, w], lo, start=False, stop=False)
                return nc.tensor.matmul(dst, w_lo[:, w], hi, start=False, stop=stop)

            def taps(lo_tap, hi_tap):
                for t in range(lo_tap, hi_tap):
                    last = split_product(CB[:], W_CONV2 + t, c1_hi[:, :, t:t + P], c1_lo[:, :, t:t + P],
                                         t == 0, t == TAPS - 1)
                return last

            def body(k, u, p, gcn, mid, conv, gate):
                q = (p + 1) % 2
                before = min(k + 2, NG) if isinstance(k, int) else k + 2
                if gate:
                    wait(pe, S["y2_done"], k + 1 if conv else NG)
                    wait(pe, S["y0_done"], before)
                    pe.wait_ge(S["xn_lo_done"], k)
                    wait(pe, S["t0_done"], before)
                    wait(pe, S["x3_done"], k + 1 if conv else NG)
                    hi, lo = ht_hi[:, q], ht_lo[:, q]
                    split_product(GR[:], W_HH, hi, lo, True, False)
                    split_product(GZ[:], W_HH + 1, hi, lo, True, False)
                    split_product(GH[:], W_HH + 2, hi, lo, True, True).then_inc(S["gate_h_done"], 1)
                    for i, dst in enumerate((GR, GZ, GI)):
                        split_product(dst[:], W_IH + 3 + i, xn_hi[:], xn_lo[:], i == 2, False)
                if conv:
                    pe.wait_ge(S["xh3_done"], k + 1)
                    wait(pe, S["ident_made"], 1)
                    wait(pe, S["adj_t_done"], before)
                    transposes(XA, xh3).then_inc(S["ht_psum"], 1)
                if gate:
                    pe.wait_ge(S["xc_lo_done"], k)
                    for i, dst in enumerate((GR, GZ, GI)):
                        last = split_product(dst[:], W_IH + i, xc_hi[:], xc_lo[:], False, True)
                    last.then_inc(S["gates_done"], 1)
                if conv:
                    pe.wait_ge(S["weights_split"], 1)
                    pe.wait_ge(S["ht_lo_done"], k + 1)
                    wait(pe, S["cv_done"], k)
                    split_product(CB[:], W_CONV1, ht_hi[:, p], ht_lo[:, p], True, True).then_inc(S["conv1_done"], 1)
                    wait(pe, S["x4_done"], k - 1)
                    split_product(XB[:], W_SE, ht_hi[:, p], ht_lo[:, p], True, True).then_inc(S["se_done"], 1)
                    wait(pe, S["ge_done"], k)
                    pe.wait_ge(S["bm3_made"], 1)
                    nc.tensor.matmul(GR[:], ones[:], bm3[:], start=True, stop=True, skip_group_check=True)
                    for g in range(G):
                        last = nc.tensor.matmul(GR[:, g], ht[:, p, g], w_raw[:, W_MSG], start=False, stop=True,
                                                skip_group_check=True)
                    last.then_inc(S["msg_psum"], 1)
                if mid:
                    pe.wait_ge(S["z1_done"], k + 2)
                    if not conv:
                        wait(pe, S["ident_made"], 1)
                    wait(pe, S["h0t_done"], before)
                    transposes(XC, z1).then_inc(S["z1t_psum"], 1)
                if conv:
                    pe.wait_ge(S["c1_lo_done"], k + 1)
                    taps(0, 2)
                if mid:
                    pe.wait_ge(S["z1t_done"], k + 2)
                    pe.wait_ge(S["w1_sum"], 1)
                    wait(pe, S["ht_hi_done"], k + 1)
                    per_graph(XC, lambda g: z1t[:, g], lambda g: w1n[:])
                    per_graph(XA, lambda g: z1t[:, g], lambda g: w1ns[:]).then_inc(S["w1_done"], 1)
                if conv:
                    taps(2, 5)
                if mid:
                    pe.wait_ge(S["y1_done"], k + 2)
                    wait(pe, S["ge_done"], k)
                    per_graph(GZ, lambda g: adj_t[:, q, g], lambda g: y1[:, g]).then_inc(S["a1_done"], 1)
                if conv:
                    taps(5, 7)
                    for name in ("dl_s", "dr_s", "dl_q", "dr_q"):
                        pe.wait_ge(S[name], k + 1)
                    per_graph(XB, lambda g: dl[:, g], lambda g: dr[:, g]).then_inc(S["dist_done"], 1)
                    taps(7, 9)
                if gcn:
                    pe.wait_ge(S["xh0_done"], k + 3)
                    wait(pe, S["y1_done"], k + 2)
                    if not mid:
                        wait(pe, S["ident_made"], 1)
                    transposes(XC, xh0).then_inc(S["h0t_psum"], 1)
                    pe.wait_ge(adj_loaded[p], (u + 2) * 16)
                    wait(pe, S["self1_done"], k + 2)
                    transposes(XA, adj_in[:, p]).then_inc(S["adj_t_psum"], 1)
                if conv:
                    pe.wait_ge(S["m3_done"], k + 1)
                    pe.wait_ge(S["msg_done"], k + 1)
                    wait(pe, S["vn_done"], k)
                    per_graph(GI, lambda g: msg[:, g], lambda g: m3[:, g]).then_inc(S["a3_done"], 1)
                    taps(9, 11)
                if gcn:
                    pe.wait_ge(S["h0t_done"], k + 3)
                    wait(pe, S["pre_done"], k + 2)
                    wait(pe, S["loads_consts"], 9 * 16)
                    per_graph(GZ, lambda g: h0t[:, g], lambda g: w0[:]).then_inc(S["w0_done"], 1)
                if conv:
                    taps(11, 12)
                if mid:
                    pe.wait_ge(S["xh2_done"], k + 2)
                    wait(pe, S["rn_done"], k)
                    transposes(GH, xh2).then_inc(S["h2t_psum"], 1)
                if gate:
                    pe.wait_ge(S["ot_done"], k)
                    wait(pe, S["ex_done"], k + 1 if conv else NG)
                    transposes(XB, ot).then_inc(S["ot_psum"], 1)
                if gcn:
                    pe.wait_ge(S["y0_done"], k + 3)
                    pe.wait_ge(S["adj_t_done"], k + 3)
                    wait(pe, S["xn_lo_done"], k + 1)
                    per_graph(GI, lambda g: adj_t[:, p, g], lambda g: y0[:, g]).then_inc(S["a0_done"], 1)
                if mid:
                    pe.wait_ge(S["h2t_done"], k + 2)
                    wait(pe, S["msg_done"], k + 1)
                    per_graph(GR, lambda g: h2t[:, g], lambda g: w2_sb[:]).then_inc(S["w2_done"], 1)
                if conv:
                    taps(12, 13)
                if mid:
                    pe.wait_ge(S["y2_done"], k + 2)
                    per_graph(GH, lambda g: adj_t[:, q, g], lambda g: y2[:, g]).then_inc(S["a2_done"], 1)
                if conv:
                    taps(13, TAPS).then_inc(S["conv2_done"], 1)

            steps(pe, body)


def kernel(**inputs):
    import numpy as np
    import concourse.bacc as bacc
    from concourse.bass_utils import run_bass_kernel_spmd

    a = {n: np.asarray(v) for n, v in inputs.items()}
    w3 = {n[len("L3_gnn_"):]: v for n, v in a.items() if n.startswith("L3_gnn_")}
    b_ih, b_hh = w3["b_ih"].reshape(3, P), w3["b_hh"].reshape(3, P)
    vecs = np.stack([a["L1_gnn_gamma"], a["L1_gnn_beta"],
                     w3["bn1_g"], w3["bn1_b"], w3["bn1_m"], w3["bn1_v"],
                     w3["bn2_g"], w3["bn2_b"], w3["bn2_m"], w3["bn2_v"],
                     b_ih[0], b_ih[1], b_ih[2], b_hh[0], b_hh[1], b_hh[2]], axis=1)
    arrays = {
        "x": a["x"], "adj": a["adj"], "mask_t": a["nodemask"].T,
        "w0_t": a["L0_gnn_W"].T, "w1_self": a["L1_gnn_W_self"], "w1_neigh": a["L1_gnn_W_neigh"],
        "w2": a["L2_gnn_weight"],
        "conv2_t": w3["conv2_w"].transpose(1, 2, 0),
        "conv1_t": w3["conv1_w"][:, :, 0].T, "msg_t": w3["w_msg"].T, "se_t": w3["w_se"].T,
        "ih_t": w3["w_ih"].reshape(3, P, 2, P).transpose(3, 2, 0, 1).reshape(P, 6, P),
        "hh_t": w3["w_hh"].reshape(3, P, P).transpose(2, 0, 1),
        "vecs": vecs, "b_se": w3["b_se"].reshape(3, 1),
        "rows": np.stack([a["L0_gnn_b"], a["L2_gnn_bias"], w3["b_msg"]]),
    }
    arrays = {n: np.ascontiguousarray(v) for n, v in arrays.items()}
    nc = bacc.Bacc("TRN2", target_bir_lowering=False, num_devices=1)
    args = [nc.dram_tensor(f"in_{n}", v.shape, mybir.dt.from_np(v.dtype), kind="ExternalInput").ap()
            for n, v in arrays.items()]
    args.append(nc.dram_tensor("out_0", (GRAPHS, P, P), mybir.dt.float32, kind="ExternalOutput").ap())
    graph_net(nc, *args)
    r = run_bass_kernel_spmd(nc, [{f"in_{n}": v for n, v in arrays.items()}], core_ids=[0])
    return r.results[0]["out_0"]
```

```python
import concourse.bass as bass
from concourse import mybir
from contextlib import ExitStack


P = 128
GRAPHS = 128
G = 4
NG = GRAPHS // G
GP = G * P
TAPS = 17
PAD = TAPS // 2
ROW = P + 2 * PAD
LN_EPS = 1e-5
EXP_LN_TABLES = 6
DEG_EPS = 1e-8

W_CONV2, W_CONV1, W_MSG, W_SE, W_IH, W_HH = 0, TAPS, TAPS + 1, TAPS + 2, TAPS + 3, TAPS + 9
NW = TAPS + 12

VECS = ["gamma", "beta", "bn1_g", "bn1_b", "bn1_m", "bn1_v", "bn2_g", "bn2_b", "bn2_m", "bn2_v",
        "b_ih_r", "b_ih_z", "b_ih_n", "b_hh_r", "b_hh_z", "b_hh_n"]


def graph_net(nc, x, adj, mask_t, w0_t, w1_self, w1_neigh, w2, conv2_t, conv1_t, msg_t, se_t, ih_t,
              hh_t, vecs, b_se, rows, out):
    f32, f32r, bf16 = mybir.dt.float32, mybir.dt.float32r, mybir.dt.bfloat16
    ALU = mybir.AluOpType
    ACT = mybir.ActivationFunctionType
    AX = mybir.AxisListType

    x_g = x.rearrange("(s g) n f -> s n g f", g=G)
    adj_g = adj.rearrange("(s g) n m -> s n g m", g=G)
    out_g = out.rearrange("(s g) n f -> s n g f", g=G)

    with ExitStack() as ctx:
        def sb(name, shape, dt=f32):
            return ctx.enter_context(nc.sbuf_tensor(name, shape, dt))

        w_raw = sb("w_raw", [P, NW, P])
        w_hi = sb("w_hi", [P, NW, P], f32r)
        w_lo = sb("w_lo", [P, NW, P], f32r)
        w0 = sb("w0", [P, P])
        w1n = sb("w1n", [P, P])
        w1s = sb("w1s", [P, P])
        w1ns = sb("w1ns", [P, P])
        w2_sb = sb("w2_sb", [P, P])
        ident = sb("ident", [P, P])
        vec = sb("vec", [P, len(VECS)])
        bnp = sb("bnp", [P, 2])
        neg_half = sb("neg_half", [P, 12])
        bns = sb("bns", [P, 2])
        bnr = sb("bnr", [P, 2])
        bnb = sb("bnb", [P, 2])
        gb = sb("gb", [P, 4])
        bse = sb("bse", [P, 1])
        b0_bc = sb("b0_bc", [P, P])
        b2_bc = sb("b2_bc", [P, P])
        bm_f = sb("bm_f", [P, P])
        bm_r = sb("bm_r", [P, P])
        bm3 = sb("bm3", [96, G, P], bf16)
        ones = sb("ones", [96, P], bf16)
        mask_sb = sb("mask_sb", [P, GRAPHS])

        x_in = sb("x_in", [P, 2, G, P])
        adj_in = sb("adj_in", [P, 2, G, P])
        adj_t = sb("adj_t", [P, 4, G, P])
        st0 = sb("st0", [P, G, 6])
        mv0 = sb("mv0", [P, G, 2])
        deg = sb("deg", [P, G])
        deg0 = sb("deg0", [P, G])
        pin0 = sb("pin0", [P, 12])
        rs0 = sb("rs0", [P, 12])
        r0d = sb("r0d", [P, G])
        nm0 = sb("nm0", [P, G])
        dm = sb("dm", [P, G])
        s_in = sb("s_in", [P, 2, G])
        cin = sb("cin", [P, 8])
        cs0 = sb("cs0", [P, G])
        crs = sb("crs", [P, 2, 8])
        ns_out = sb("ns_out", [P, G])
        xh0 = sb("xh0", [P, G, P])
        h0t = sb("h0t", [P, G, P])
        y0 = sb("y0", [P, G, P])
        t0 = sb("t0", [P, G, P])
        u0 = sb("u0", [P, G, P])
        x1 = sb("x1", [P, G, P])

        st1 = sb("st1", [P, G, 6])
        mv1 = sb("mv1", [P, G, 2])
        e1 = sb("e1", [P, G])
        cc = sb("cc", [P, G, P])
        stc = sb("stc", [P, G, 6])
        mvc = sb("mvc", [P, G, 2])
        pin1 = sb("pin1", [P, G])
        q1 = sb("q1", [P, G])
        nmq = sb("nmq", [P, G])
        z1 = sb("z1", [P, G, P])
        z1t = sb("z1t", [P, G, P])
        y1 = sb("y1", [P, G, P])
        self1 = sb("self1", [P, G, P])
        pre = sb("pre", [P, G, P])
        sp_a = sb("sp_a", [P, G, P])
        sp_e = sb("sp_e", [P, G, P])
        sp_l = sb("sp_l", [P, G, P])
        sp = sb("sp", [P, G, P])
        x2 = sb("x2", [P, G, P])
        x2b = sb("x2b", [P, G, P])
        st2 = sb("st2", [P, G, 6])
        mv2 = sb("mv2", [P, G, 2])
        pin2 = sb("pin2", [P, G])
        rs2 = sb("rs2", [P, G])
        r2d = sb("r2d", [P, G])
        h2 = sb("h2", [P, G, P])
        nm2 = sb("nm2", [P, G])
        z2t = sb("z2t", [P, G, P])
        x3 = sb("x3", [P, 4, G, P])
        st3 = sb("st3", [P, G, 6])
        mv3 = sb("mv3", [P, G, 2])
        pin3 = sb("pin3", [P, G])
        rs3 = sb("rs3", [P, G])
        nm3 = sb("nm3", [P, G])
        xh3 = sb("xh3", [P, G, P])

        ht = sb("ht", [P, 2, G, P])
        ht_hi = sb("ht_hi", [P, 2, G, P], f32r)
        ht_lo = sb("ht_lo", [P, 2, G, P], f32r)
        htb = sb("htb", [P, G, P])
        c1 = sb("c1", [P, G, P])
        c1_hi = sb("c1_hi", [P, G, ROW], f32r)
        c1_lo = sb("c1_lo", [P, G, ROW], f32r)
        msg = sb("msg", [P, G, P])
        dl = sb("dl", [96, G, P])
        dr = sb("dr", [96, G, P])
        ex = sb("ex", [P, G, P])
        m3 = sb("m3", [P, G, P])
        xn_hi = sb("xn_hi", [P, G, P], f32r)
        xn_lo = sb("xn_lo", [P, G, P], f32r)

        cv = sb("cv", [P, G, P])
        xc_hi = sb("xc_hi", [P, G, P], f32r)
        xc_lo = sb("xc_lo", [P, G, P], f32r)
        ge = sb("ge", [P, 2, GP])
        gl = sb("gl", [P, 2, GP])
        rz = sb("rz", [P, 2, GP])
        rn = sb("rn", [P, GP])
        vn = sb("vn", [P, GP])
        ne = sb("ne", [P, GP])
        nl = sb("nl", [P, GP])
        nq = sb("nq", [P, GP])
        nn = sb("nn", [P, GP])
        hd = sb("hd", [P, GP])
        zd = sb("zd", [P, GP])
        ot = sb("ot", [P, G, P])
        x4 = sb("x4", [P, 2, G, P])

        def bank(name):
            return ctx.enter_context(nc.psum_tensor(name, [P, G, P], f32))

        CB = bank("bank_conv")
        GR, GZ, GI, GH = bank("bank_r"), bank("bank_z"), bank("bank_in"), bank("bank_hn")
        XA, XB, XC = bank("bank_a"), bank("bank_b"), bank("bank_c")

        def flat(t):
            return t.rearrange("p g n -> p (g n)")

        names = """
            loads_weights loads_consts ident_zero ident_made halves_set bn_in bn_pow bn_scale bn_shift
            weights_hi weights_split se_zero gate_bias pads_set bm_hi bm_r1 bm_mid bm_r2 bm3_made w1_sum
            x_loaded_0 x_loaded_1 adj_loaded_0 adj_loaded_1 x_stored_0 x_stored_1
            st0_done mv0_done deg_done deg0_done pin0_done rs0_done r0d_done nm0_done dm_done xh0_done
            adj_t_psum adj_t_done h0t_psum h0t_done cs0_done is0_done cin_done crs_done ns_done
            w0_done y0_done a0_done t0_done u0_done x1_done
            st1_done mv1_done e1_done c_done stc_done mvc_done pin1_done q1_done nmq_done z1_done z1b_done
            z1t_psum z1t_done w1_done y1_done self1_done a1_done pre_done spa_done spe_done spl_done
            sp_done x2_done x2b_done st2_done mv2_done pin2_done rs2_done r2d_done nm2_done h2_done
            a2_done z2t_done w2_done x3_done st3_done mv3_done pin3_done rs3_done nm3_done
            xh3_done
            ht_psum ht_done ht_hi_done ht_lo_done htb_done conv1_done c1_done c1_hi_done c1_lo_done
            se_done dl_s dr_s dl_q dr_q msg_psum msg_done dist_done ex_done m3_done
            a3_done xn_hi_done xn_lo_done conv2_done
            cv_done xc_hi_done xc_lo_done gate_h_done gates_done gez_done ge_done gl_done rz_done rn_done vn_done
            ne_done nl_done nq_done nn_done hd_done zd_done ot_done ot_psum x4_done
            tick_dve tick_sp
        """.split()
        S = {n: ctx.enter_context(nc.semaphore(n)) for n in names}

        x_loaded, adj_loaded = (S["x_loaded_0"], S["x_loaded_1"]), (S["adj_loaded_0"], S["adj_loaded_1"])
        x_stored = (S["x_stored_0"], S["x_stored_1"])

        def wait(eng, sem, n):
            if not isinstance(n, int):
                eng.wait_ge(sem, n)
            elif n > 0:
                eng.wait_ge(sem, min(n, NG))

        def steps(eng, body):
            def peeled(k):
                body(k, k // 2, k % 4, *(0 <= k + ahead < NG for ahead in (3, 2, 1, 0, -1)))

            for k in range(-3, 4):
                peeled(k)
            with eng.Fori(1, NG // 4 - 1) as j:
                for s in range(4):
                    body(j * 4 + s, j * 2 + s // 2, s, True, True, True, True, True)
            for k in range(NG - 4, NG + 1):
                peeled(k)

        block = ctx.enter_context(nc.Block())

        @block.sync
        def _(sp):
            n_w = 0
            for dst, src in ((w0[:], w0_t), (w1n[:], w1_neigh), (w1s[:], w1_self), (w2_sb[:], w2),
                             (vec[:], vecs), (mask_sb[:], mask_t),
                             (b0_bc[:], rows[0:1, :].broadcast_to([P, P])),
                             (b2_bc[:], rows[1:2, :].broadcast_to([P, P])),
                             (bm_f[:], rows[2:3, :].broadcast_to([P, P]))):
                sp.dma_start(dst, src).then_inc(S["loads_consts"], 16)
                n_w += 1
            assert n_w == 9

            def load(g, slot):
                wait(sp, S["x1_done"], g - 1)
                sp.sem_inc(S["tick_sp"], 1)
                sp.dma_start(x_in[:, slot], x_g[g]).then_inc(x_loaded[slot], 16)
                wait(sp, S["deg_done"], g - 1)
                sp.sem_inc(S["tick_sp"], 1)
                wait(sp, S["adj_t_psum"], g - 1)
                sp.sem_inc(S["tick_sp"], 1)
                sp.dma_start(adj_in[:, slot], adj_g[g]).then_inc(adj_loaded[slot], 16)

            def load_weights():
                sp.wait_ge(S["se_zero"], 2)
                sp.dma_start(w_raw[:, W_CONV2:W_CONV2 + TAPS, :], conv2_t).then_inc(S["loads_weights"], 16)
                sp.dma_start(w_raw[:, W_CONV1, :], conv1_t).then_inc(S["loads_weights"], 16)
                sp.dma_start(w_raw[:, W_MSG, :], msg_t).then_inc(S["loads_weights"], 16)
                sp.dma_start(w_raw[:, W_IH:W_IH + 6, :], ih_t).then_inc(S["loads_weights"], 16)
                sp.dma_start(w_raw[:, W_HH:W_HH + 3, :], hh_t).then_inc(S["loads_weights"], 16)
                for r in range(3):
                    sp.dma_start(w_raw[:, W_SE, 32 * r:32 * r + 3], se_t).then_inc(S["loads_weights"], 16)
                    sp.dma_start(bse[32 * r:32 * r + 3, 0:1], b_se).then_inc(S["loads_weights"], 16)

            def body(k, u, s, prep, gcn, mid, conv, gate):
                if prep:
                    load(k + 3, (s + 1) % 2)
                if isinstance(k, int) and k == -2:
                    load_weights()
                if gate:
                    wait(sp, S["x4_done"], k)
                    sp.sem_inc(S["tick_sp"], 1)
                    sp.dma_start(out_g[k - 1], x4[:, (s + 1) % 2]).then_inc(x_stored[(s + 1) % 2], 16)

            steps(sp, body)
            sp.wait_ge(S["x_stored_0"], 16 * NG // 2)
            sp.wait_ge(S["x_stored_1"], 16 * NG // 2)

        @block.gpsimd
        def _(pool):
            nc.gpsimd.memset(w_raw[:, W_SE, :], 0.0).then_inc(S["se_zero"], 1)
            nc.gpsimd.memset(bse[:], 0.0).then_inc(S["se_zero"], 1)
            nc.gpsimd.memset(neg_half[:], -0.5).then_inc(S["halves_set"], 1)
            nc.gpsimd.memset(ident[:], 0.0).then_inc(S["ident_zero"], 1)
            pool.wait_ge(S["ident_zero"], 1)
            nc.gpsimd.affine_select(out=ident[:], in_=ident[:], compare_op=ALU.not_equal, fill=1.0, base=0,
                                    pattern=[[-1, P]], channel_multiplier=1).then_inc(S["ident_made"], 1)
            pool.wait_ge(S["halves_set"], 1)
            pool.wait_ge(S["bn_in"], 1)
            nc.gpsimd.tensor_tensor(bnr[:], bnp[:], neg_half[:, 0:2], ALU.pow).then_inc(S["bn_pow"], 1)
            nc.gpsimd.memset(c1_hi[:].bitcast(f32), 0.0).then_inc(S["pads_set"], 1)
            nc.gpsimd.memset(c1_lo[:].bitcast(f32), 0.0).then_inc(S["pads_set"], 1)

            def body(k, u, s, prep, gcn, mid, conv, gate):
                p, q = s % 2, (s + 1) % 2
                if conv:
                    wait(pool, S["ht_done"], k + 1)
                    wait(pool, S["bn_shift"], 1)
                    wait(pool, S["cv_done"], k)
                    nc.gpsimd.tensor_tensor(htb[:], ht[:, p], bnb[:, 1:2].unsqueeze(2).broadcast_to([P, G, P]),
                                            ALU.add).then_inc(S["htb_done"], 1)
                if mid:
                    wait(pool, S["pin2_done"], k + 2)
                    nc.gpsimd.tensor_tensor(rs2[:], pin2[:], neg_half[:, 0:G], ALU.pow).then_inc(S["rs2_done"], 1)
                    wait(pool, S["loads_consts"], 9 * 16)
                    wait(pool, S["x2_done"], k + 2)
                    wait(pool, S["x3_done"], k + 1)
                    nc.gpsimd.tensor_tensor(x2b[:], x2[:], b2_bc[:].unsqueeze(1).broadcast_to([P, G, P]),
                                            ALU.add).then_inc(S["x2b_done"], 1)
                if prep:
                    wait(pool, S["pin0_done"], k + 4)
                    wait(pool, S["dm_done"], k + 3)
                    wait(pool, S["y0_done"], k + 3)
                    nc.gpsimd.tensor_tensor(rs0[:], pin0[:], neg_half[:, 0:12], ALU.pow).then_inc(S["rs0_done"], 1)
                if gcn:
                    wait(pool, S["cin_done"], k + 3)
                    wait(pool, S["x3_done"], k + 1)
                    nc.gpsimd.tensor_tensor(crs[:, p], cin[:], neg_half[:, 0:8], ALU.pow).then_inc(S["crs_done"], 1)
                if conv:
                    wait(pool, S["ex_done"], k + 1)
                    wait(pool, S["adj_t_done"], k + 1)
                    wait(pool, S["a3_done"], k)
                    nc.gpsimd.tensor_tensor(m3[:], ex[:], adj_t[:, s], ALU.mult).then_inc(S["m3_done"], 1)
                if gcn:
                    wait(pool, S["pin1_done"], k + 3)
                    wait(pool, S["z1_done"], k + 2)
                    wait(pool, S["z1b_done"], k + 2)
                    nc.gpsimd.tensor_tensor(q1[:], pin1[:], neg_half[:, 0:G], ALU.pow).then_inc(S["q1_done"], 1)
                if gate:
                    wait(pool, S["nn_done"], k)
                    wait(pool, S["ht_done"], k)
                    nc.gpsimd.tensor_tensor(hd[:], flat(ht[:, q]), nn[:], ALU.subtract).then_inc(S["hd_done"], 1)
                    wait(pool, S["rz_done"], k)
                    wait(pool, S["hd_done"], k)
                    nc.gpsimd.tensor_tensor(zd[:], hd[:], rz[:, 1], ALU.mult).then_inc(S["zd_done"], 1)
                    wait(pool, S["zd_done"], k)
                    wait(pool, S["ot_psum"], k - 1)
                    nc.gpsimd.tensor_tensor(flat(ot[:]), zd[:], nn[:], ALU.add).then_inc(S["ot_done"], 1)
                if mid:
                    wait(pool, S["pin3_done"], k + 2)
                    wait(pool, S["xh3_done"], k + 1)
                    nc.gpsimd.tensor_tensor(rs3[:], pin3[:], neg_half[:, 0:G], ALU.pow).then_inc(S["rs3_done"], 1)

            steps(pool, body)

        @block.scalar
        def _(act):
            nc.scalar.add_instruction(mybir.InstLoadActFuncSet(
                name=nc.get_next_instruction_name(), engine=mybir.EngineType.Activation, act_func_set_id=EXP_LN_TABLES))

            def scaled(dst, src, scale, shift, sem, func=ACT.Identity, graphs=G):
                for g in range(graphs):
                    last = nc.scalar.activation(dst[:, g], src[:, g], func, bias=shift[:, g:g + 1],
                                                scale=scale[:, g:g + 1])
                last.then_inc(sem, 1)

            def body(k, u, s, prep, gcn, mid, conv, gate):
                p, q = s % 2, (s + 1) % 2
                if mid:
                    act.wait_ge(S["pre_done"], k + 2)
                    nc.scalar.activation(sp_a[:], pre[:], ACT.Abs).then_inc(S["spa_done"], 1)
                if conv:
                    act.wait_ge(S["ht_psum"], k + 1)
                    wait(act, S["hd_done"], k - 1)
                    nc.scalar.activation(ht[:, p], XA[:], ACT.Relu).then_inc(S["ht_done"], 1)
                    wait(act, S["gate_h_done"], k - 1)
                    nc.scalar.activation(ht_hi[:, p], XA[:], ACT.Relu).then_inc(S["ht_hi_done"], 1)
                if gate:
                    act.wait_ge(S["cv_done"], k)
                    wait(act, S["gates_done"], k - 1)
                    nc.scalar.activation(xc_hi[:], cv[:], ACT.Relu).then_inc(S["xc_hi_done"], 1)
                if mid:
                    act.wait_ge(S["spa_done"], k + 2)
                    nc.scalar.activation(sp_e[:], sp_a[:], ACT.Exp, scale=-1.0).then_inc(S["spe_done"], 1)
                    act.wait_ge(S["spe_done"], k + 2)
                    wait(act, S["sp_done"], k + 1)
                    nc.scalar.activation(sp_l[:], sp_e[:], ACT.Ln, bias=1.0).then_inc(S["spl_done"], 1)
                if gcn:
                    act.wait_ge(S["h0t_psum"], k + 3)
                    wait(act, S["w0_done"], k + 2)
                    nc.scalar.activation(h0t[:], XA[:], ACT.Relu).then_inc(S["h0t_done"], 1)
                if conv:
                    act.wait_ge(S["conv1_done"], k + 1)
                    act.wait_ge(S["bn_shift"], 1)
                    wait(act, S["c1_lo_done"], k)
                    nc.scalar.activation(c1[:], CB[:], ACT.Relu, bias=bnb[:, 0:1],
                                         scale=bns[:, 0:1]).then_inc(S["c1_done"], 1)
                    act.wait_ge(S["pads_set"], 5)
                    wait(act, S["conv2_done"], k)
                    nc.scalar.activation(c1_hi[:, :, PAD:PAD + P], CB[:], ACT.Relu, bias=bnb[:, 0:1],
                                         scale=bns[:, 0:1]).then_inc(S["c1_hi_done"], 1)
                if conv:
                    act.wait_ge(S["se_done"], k + 1)
                    act.wait_ge(S["loads_weights"], 11 * 16)
                    wait(act, S["dist_done"], k)
                    nc.scalar.activation(dl[0:32], XB[0:32], ACT.Identity, bias=bse[0:32, 0:1]).then_inc(S["dl_s"], 1)
                    nc.scalar.activation(dl[32:64], XB[32:64], ACT.Square, bias=bse[32:64, 0:1]).then_inc(S["dl_q"], 1)
                if gate:
                    act.wait_ge(S["gates_done"], k)
                    act.wait_ge(S["gate_bias"], 3)
                    wait(act, S["gl_done"], k - 1)
                    nc.scalar.activation(ge[:, 1], flat(GZ[:]), ACT.Exp, bias=gb[:, 1:2],
                                         scale=-1.0).then_inc(S["gez_done"], 1)
                    nc.scalar.activation(ge[:, 0], flat(GR[:]), ACT.Exp, bias=gb[:, 0:1],
                                         scale=-1.0).then_inc(S["ge_done"], 1)
                if conv:
                    wait(act, S["dist_done"], k)
                    nc.scalar.activation(dr[64:96], XB[64:96], ACT.Square, bias=bse[64:96, 0:1]).then_inc(S["dr_q"], 1)
                if gcn:
                    act.wait_ge(S["adj_t_psum"], k + 3)
                    wait(act, S["m3_done"], k - 1)
                    wait(act, S["crs_done"], k + 2)
                    for g in range(G):
                        last = nc.scalar.activation(adj_t[:, (s + 2) % 4, g], GZ[:, g], ACT.Copy,
                                                    accum_out=cin[:, g:g + 1])
                    last.then_inc(S["adj_t_done"], 1)
                if gate:
                    act.wait_ge(S["ge_done"], k)
                    nc.scalar.activation(gl[:], ge[:], ACT.Ln, bias=1.0).then_inc(S["gl_done"], 1)
                if gate:
                    act.wait_ge(S["gl_done"], k)
                    wait(act, S["rn_done"], k - 1)
                    wait(act, S["zd_done"], k - 1)
                    nc.scalar.activation(rz[:], gl[:], ACT.Exp, scale=-1.0).then_inc(S["rz_done"], 1)
                if conv:
                    act.wait_ge(S["msg_psum"], k + 1)
                    wait(act, S["a3_done"], k)
                    nc.scalar.activation(msg[:], GR[:], ACT.Relu).then_inc(S["msg_done"], 1)
                if mid:
                    act.wait_ge(S["nm2_done"], k + 2)
                    wait(act, S["a2_done"], k + 1)
                    scaled(h2, x2, r2d, nm2, S["h2_done"], ACT.Relu)
                if conv:
                    act.wait_ge(S["dist_done"], k + 1)
                    wait(act, S["m3_done"], k)
                    nc.scalar.activation(ex[:], XB[:], ACT.Exp).then_inc(S["ex_done"], 1)
                if mid:
                    act.wait_ge(S["a2_done"], k + 2)
                    wait(act, S["w2_done"], k + 1)
                    nc.scalar.activation(z2t[:], GR[:], ACT.Copy).then_inc(S["z2t_done"], 1)
                if gate:
                    act.wait_ge(S["vn_done"], k)
                    wait(act, S["nl_done"], k - 1)
                    nc.scalar.activation(ne[:], vn[:], ACT.Exp, bias=gb[:, 3:4], scale=-2.0).then_inc(S["ne_done"], 1)
                if gate:
                    act.wait_ge(S["ne_done"], k)
                    nc.scalar.activation(nl[:], ne[:], ACT.Ln, bias=1.0).then_inc(S["nl_done"], 1)
                    act.wait_ge(S["nl_done"], k)
                    wait(act, S["nn_done"], k - 1)
                    nc.scalar.activation(nq[:], nl[:], ACT.Exp, scale=-1.0).then_inc(S["nq_done"], 1)
                if conv:
                    act.wait_ge(S["a3_done"], k + 1)
                    wait(act, S["gates_done"], k)
                    nc.scalar.activation(xn_hi[:], GI[:], ACT.Copy).then_inc(S["xn_hi_done"], 1)
                if gcn:
                    act.wait_ge(S["nmq_done"], k + 3)
                    act.wait_ge(S["q1_done"], k + 3)
                    wait(act, S["z1t_psum"], k + 2)
                    scaled(z1, cc, q1, nmq, S["z1_done"], graphs=G // 2)
                if gcn:
                    act.wait_ge(S["z1t_psum"], k + 3)
                    act.wait_ge(S["loads_consts"], 9 * 16)
                    wait(act, S["w1_done"], k + 2)
                    nc.scalar.activation(z1t[:], XA[:], ACT.Identity, bias=vec[:, 1:2],
                                         scale=vec[:, 0:1]).then_inc(S["z1t_done"], 1)
                if prep:
                    act.wait_ge(S["nm0_done"], k + 4)
                    act.wait_ge(x_loaded[q], (u + 2 + p) * 16)
                    wait(act, S["h0t_psum"], k + 3)
                    scaled(xh0, x_in[:, q], r0d, nm0, S["xh0_done"])
                if gcn:
                    act.wait_ge(S["w1_done"], k + 3)
                    wait(act, S["pre_done"], k + 2)
                    nc.scalar.activation(self1[:], GH[:], ACT.Copy).then_inc(S["self1_done"], 1)
                if mid:
                    act.wait_ge(S["nm3_done"], k + 2)
                    wait(act, S["ht_psum"], k + 1)
                    scaled(xh3, x3[:, (s + 1) % 4], rs3, nm3, S["xh3_done"])

            steps(act, body)

        @block.vector
        def _(dve):
            nc.vector.memset(dl[64:96], -1.0).then_inc(S["pads_set"], 1)
            nc.vector.memset(dr[32:64], -1.0).then_inc(S["pads_set"], 1)
            nc.vector.memset(ones[:], 1.0 / 32).then_inc(S["pads_set"], 1)
            dve.wait_ge(S["loads_consts"], 9 * 16)
            nc.vector.tensor_tensor(w1ns[:], w1s[:], w1n[:], ALU.add).then_inc(S["w1_sum"], 1)
            for i in range(2):
                last = nc.vector.tensor_scalar(bnp[:, i:i + 1], vec[:, 5 + 4 * i:6 + 4 * i], LN_EPS, None, ALU.add)
            last.then_inc(S["bn_in"], 1)
            nc.vector.tensor_copy(bm3[:, 0], bm_f[0:96]).then_inc(S["bm_hi"], 1)
            dve.wait_ge(S["bm_hi"], 1)
            nc.vector.tensor_tensor(bm_r[0:96], bm_f[0:96], bm3[:, 0], ALU.subtract).then_inc(S["bm_r1"], 1)
            dve.wait_ge(S["bm_r1"], 1)
            nc.vector.tensor_copy(bm3[32:64, 0], bm_r[32:64])
            nc.vector.tensor_copy(bm3[64:96, 0], bm_r[64:96]).then_inc(S["bm_mid"], 1)
            dve.wait_ge(S["bm_mid"], 1)
            nc.vector.tensor_tensor(bm_f[64:96], bm_r[64:96], bm3[64:96, 0], ALU.subtract).then_inc(S["bm_r2"], 1)
            dve.wait_ge(S["bm_r2"], 1)
            nc.vector.tensor_copy(bm3[64:96, 0], bm_f[64:96]).then_inc(S["bm_mid"], 1)
            dve.wait_ge(S["bm_mid"], 2)
            for g in range(1, G):
                last = nc.vector.tensor_copy(bm3[:, g], bm3[:, 0])
            last.then_inc(S["bm3_made"], 1)
            nc.vector.tensor_tensor(gb[:, 0:2], vec[:, 10:12], vec[:, 13:15], ALU.add).then_inc(S["gate_bias"], 1)
            dve.wait_ge(S["gate_bias"], 1)
            nc.vector.tensor_scalar(gb[:, 0:2], gb[:, 0:2], -1.0, None, ALU.mult).then_inc(S["gate_bias"], 1)
            nc.vector.tensor_scalar(gb[:, 3:4], vec[:, 12:13], -2.0, None, ALU.mult).then_inc(S["gate_bias"], 1)
            dve.wait_ge(S["bn_pow"], 1)
            for i in range(2):
                last = nc.vector.tensor_tensor(bns[:, i:i + 1], bnr[:, i:i + 1], vec[:, 2 + 4 * i:3 + 4 * i], ALU.mult)
            last.then_inc(S["bn_scale"], 1)
            dve.wait_ge(S["bn_scale"], 1)
            for i in range(2):
                last = nc.vector.tensor_tensor(bnr[:, i:i + 1], bns[:, i:i + 1], vec[:, 4 + 4 * i:5 + 4 * i], ALU.mult)
            last.then_inc(S["bn_scale"], 1)
            dve.wait_ge(S["bn_scale"], 2)
            for i in range(2):
                last = nc.vector.tensor_tensor(bnb[:, i:i + 1], vec[:, 3 + 4 * i:4 + 4 * i], bnr[:, i:i + 1], ALU.subtract)
            last.then_inc(S["bn_shift"], 1)

            def split_weights():
                dve.wait_ge(S["loads_weights"], 11 * 16)
                nc.vector.tensor_copy(w_hi[:], w_raw[:]).then_inc(S["weights_hi"], 1)
                dve.wait_ge(S["weights_hi"], 1)
                nc.vector.tensor_tensor(w_lo[:], w_raw[:], w_hi[:].bitcast(f32), ALU.subtract).then_inc(S["weights_split"], 1)

            def bn(src, st, sem):
                for g in range(G):
                    last = nc.vector.bn_stats(st[:, g], src[:, g])
                last.then_inc(sem, 1)

            def aggregate(st, mv, sem):
                dve.sem_inc(S["tick_dve"], 1)
                for g in range(G):
                    last = nc.vector.bn_aggr(mv[:, g], st[:, g])
                last.then_inc(sem, 1)

            def stats(src, st, mv, st_sem, mv_sem, n):
                bn(src, st, st_sem)
                dve.wait_ge(st_sem, n)
                aggregate(st, mv, mv_sem)
                dve.wait_ge(mv_sem, n)

            def body(k, u, s, prep, gcn, mid, conv, gate):
                p, q = s % 2, (s + 1) % 2
                if isinstance(k, int) and k == -2:
                    split_weights()
                if gate:
                    dve.wait_ge(S["conv2_done"], k)
                    dve.wait_ge(S["htb_done"], k)
                    nc.vector.scalar_tensor_tensor(cv[:], CB[:], bns[:, 1:2], htb[:], ALU.mult,
                                                   ALU.add).then_inc(S["cv_done"], 1)
                if conv:
                    dve.wait_ge(S["ht_hi_done"], k + 1)
                    wait(dve, S["gate_h_done"], k - 1)
                    nc.vector.tensor_tensor(ht_lo[:, p], ht[:, p], ht_hi[:, p].bitcast(f32),
                                            ALU.subtract).then_inc(S["ht_lo_done"], 1)
                if gate:
                    dve.wait_ge(S["xc_hi_done"], k)
                    nc.vector.scalar_tensor_tensor(xc_lo[:], cv[:], 0.0, xc_hi[:].bitcast(f32), ALU.max,
                                                   ALU.subtract).then_inc(S["xc_lo_done"], 1)
                if mid:
                    dve.wait_ge(S["spl_done"], k + 2)
                    nc.vector.scalar_tensor_tensor(sp[:], pre[:], 0.0, sp_l[:], ALU.max, ALU.add).then_inc(S["sp_done"], 1)
                    dve.wait_ge(S["sp_done"], k + 2)
                    wait(dve, S["x2b_done"], k + 1)
                    wait(dve, S["h2_done"], k + 1)
                    nc.vector.tensor_tensor(x2[:], x1[:], sp[:], ALU.add).then_inc(S["x2_done"], 1)
                    dve.wait_ge(S["x2_done"], k + 2)
                    stats(x2, st2, mv2, S["st2_done"], S["mv2_done"], k + 2)
                    nc.vector.tensor_scalar(pin2[:], mv2[:, :, 1], LN_EPS, None, ALU.add).then_inc(S["pin2_done"], 1)
                if conv:
                    dve.wait_ge(S["c1_hi_done"], k + 1)
                    nc.vector.tensor_tensor(c1_lo[:, :, PAD:PAD + P], c1[:], c1_hi[:, :, PAD:PAD + P].bitcast(f32),
                                            ALU.subtract).then_inc(S["c1_lo_done"], 1)
                if conv:
                    dve.wait_ge(S["dl_s"], k + 1)
                    wait(dve, S["dist_done"], k)
                    nc.vector.tensor_scalar(dr[0:32], dl[0:32], 2.0, None, ALU.mult).then_inc(S["dr_s"], 1)
                if prep:
                    dve.wait_ge(adj_loaded[q], (u + 2 + p) * 16)
                    wait(dve, S["rs0_done"], k + 3)
                    nc.vector.tensor_reduce(deg[:], adj_in[:, q], AX.X, ALU.add).then_inc(S["deg_done"], 1)
                    dve.wait_ge(S["deg_done"], k + 4)
                    nc.vector.tensor_scalar(deg0[:], deg[:], 0.0, None, ALU.is_equal).then_inc(S["deg0_done"], 1)
                    nc.vector.tensor_scalar(pin0[:, 4:8], deg[:], 1.0, DEG_EPS, ALU.add, ALU.add)
                if mid:
                    dve.wait_ge(S["rs2_done"], k + 2)
                    wait(dve, S["h2_done"], k + 1)
                    nc.vector.tensor_tensor(r2d[:], rs2[:], crs[:, q, 0:4], ALU.mult).then_inc(S["r2d_done"], 1)
                    dve.wait_ge(S["r2d_done"], k + 2)
                    nc.vector.scalar_tensor_tensor(nm2[:], mv2[:, :, 0], -1.0, r2d[:], ALU.mult,
                                                   ALU.mult).then_inc(S["nm2_done"], 1)
                if gcn:
                    dve.wait_ge(S["w0_done"], k + 3)
                    wait(dve, S["a0_done"], k + 2)
                    for g in range(G):
                        last = nc.vector.scalar_tensor_tensor(y0[:, g], b0_bc[:], rs0[:, 4 + g:5 + g], XA[:, g],
                                                              ALU.mult, ALU.add)
                    last.then_inc(S["y0_done"], 1)
                if prep:
                    dve.wait_ge(x_loaded[q], (u + 2 + p) * 16)
                    stats(x_in[:, q], st0, mv0, S["st0_done"], S["mv0_done"], k + 4)
                    nc.vector.tensor_scalar(pin0[:, 0:4], mv0[:, :, 1], LN_EPS, None, ALU.add)
                    dve.wait_ge(S["deg0_done"], k + 4)
                    nc.vector.tensor_tensor(pin0[:, 8:12], deg[:], deg0[:], ALU.add).then_inc(S["pin0_done"], 1)
                if gcn:
                    dve.wait_ge(S["adj_t_done"], k + 3)
                    nc.vector.tensor_scalar(cs0[:], cin[:, 0:4], 0.0, None, ALU.is_equal).then_inc(S["cs0_done"], 1)
                    dve.wait_ge(S["cs0_done"], k + 3)
                    wait(dve, S["crs_done"], k + 2)
                    nc.vector.tensor_tensor(cin[:, 4:8], cin[:, 0:4], cs0[:], ALU.add).then_inc(S["cin_done"], 1)
                if gcn:
                    dve.wait_ge(S["a0_done"], k + 3)
                    wait(dve, S["u0_done"], k + 2)
                    nc.vector.tensor_tensor(t0[:], GZ[:], y0[:], ALU.add).then_inc(S["t0_done"], 1)
                    dve.wait_ge(S["t0_done"], k + 3)
                    dve.wait_ge(S["dm_done"], k + 3)
                    for g in range(G):
                        last = nc.vector.tensor_scalar(u0[:, g], t0[:, g], dm[:, g:g + 1], 0.0, ALU.mult, ALU.max)
                    last.then_inc(S["u0_done"], 1)
                    dve.wait_ge(S["u0_done"], k + 3)
                    dve.wait_ge(x_loaded[p], (u + 2) * 16)
                    wait(dve, S["x2_done"], k + 2)
                    wait(dve, S["c_done"], k + 2)
                    nc.vector.tensor_tensor(x1[:], x_in[:, p], u0[:], ALU.add).then_inc(S["x1_done"], 1)
                    dve.wait_ge(S["x1_done"], k + 3)
                    bn(x1, st1, S["st1_done"])
                if gate:
                    dve.wait_ge(S["rz_done"], k)
                    nc.vector.scalar_tensor_tensor(rn[:], flat(GH[:]), vec[:, 15:16], rz[:, 0], ALU.add,
                                                   ALU.mult).then_inc(S["rn_done"], 1)
                    dve.wait_ge(S["rn_done"], k)
                    wait(dve, S["ne_done"], k - 1)
                    nc.vector.tensor_tensor(vn[:], flat(GI[:]), rn[:], ALU.add).then_inc(S["vn_done"], 1)
                if gcn:
                    dve.wait_ge(S["crs_done"], k + 3)
                    nc.vector.scalar_tensor_tensor(ns_out[:], cs0[:], -1.0, crs[:, p, 4:8], ALU.add,
                                                   ALU.mult).then_inc(S["ns_done"], 1)
                if prep:
                    dve.wait_ge(S["rs0_done"], k + 4)
                    wait(dve, S["xh0_done"], k + 3)
                    nc.vector.tensor_tensor(r0d[:], rs0[:, 0:4], rs0[:, 4:8], ALU.mult).then_inc(S["r0d_done"], 1)
                    nc.vector.tensor_scalar(deg0[:], deg0[:], -1.0, 1.0, ALU.mult, ALU.add).then_inc(S["is0_done"], 1)
                if gcn:
                    dve.wait_ge(S["st1_done"], k + 3)
                    aggregate(st1, mv1, S["mv1_done"])
                if prep:
                    dve.wait_ge(S["r0d_done"], k + 4)
                    nc.vector.scalar_tensor_tensor(nm0[:], mv0[:, :, 0], -1.0, r0d[:], ALU.mult,
                                                   ALU.mult).then_inc(S["nm0_done"], 1)
                    dve.wait_ge(S["is0_done"], k + 4)
                    nc.vector.tensor_tensor(s_in[:, q], rs0[:, 8:12], deg0[:], ALU.mult)
                    mask_cols = mask_sb[:, bass.ds((k + 3) * G, G)] if not isinstance(k, int) else \
                        mask_sb[:, (k + 3) * G:(k + 4) * G]
                    wait(dve, S["u0_done"], k + 3)
                    nc.vector.tensor_tensor(dm[:], rs0[:, 4:8], mask_cols, ALU.mult).then_inc(S["dm_done"], 1)
                if gcn:
                    dve.wait_ge(S["mv1_done"], k + 3)
                    nc.vector.tensor_scalar(e1[:], mv1[:, :, 1], LN_EPS, LN_EPS, ALU.add, ALU.mult).then_inc(S["e1_done"], 1)
                    wait(dve, S["z1_done"], k + 2)
                    for g in range(G):
                        last = nc.vector.tensor_scalar(cc[:, g], x1[:, g], mv1[:, g, 0:1], mv1[:, g, 0:1],
                                                       ALU.max, ALU.subtract)
                    last.then_inc(S["c_done"], 1)
                if gcn:
                    dve.wait_ge(S["c_done"], k + 3)
                    stats(cc, stc, mvc, S["stc_done"], S["mvc_done"], k + 3)
                    dve.wait_ge(S["e1_done"], k + 3)
                    nc.vector.tensor_tensor(pin1[:], mvc[:, :, 1], e1[:], ALU.add).then_inc(S["pin1_done"], 1)
                if gate:
                    dve.wait_ge(S["nq_done"], k)
                    wait(dve, S["ot_done"], k - 1)
                    nc.vector.tensor_scalar(nn[:], nq[:], 2.0, -1.0, ALU.mult, ALU.add).then_inc(S["nn_done"], 1)
                if gcn:
                    dve.wait_ge(S["q1_done"], k + 3)
                    nc.vector.scalar_tensor_tensor(nmq[:], mvc[:, :, 0], -1.0, q1[:], ALU.mult,
                                                   ALU.mult).then_inc(S["nmq_done"], 1)
                    dve.wait_ge(S["nmq_done"], k + 3)
                    wait(dve, S["z1t_psum"], k + 2)
                    for g in range(G // 2, G):
                        last = nc.vector.tensor_scalar(z1[:, g], cc[:, g], q1[:, g:g + 1], nmq[:, g:g + 1],
                                                       ALU.mult, ALU.add)
                    last.then_inc(S["z1b_done"], 1)
                if mid:
                    dve.wait_ge(S["w2_done"], k + 2)
                    dve.wait_ge(S["x2b_done"], k + 2)
                    wait(dve, S["x4_done"], k - 2)
                    for g in range(G):
                        last = nc.vector.scalar_tensor_tensor(x3[:, (s + 1) % 4, g], XC[:, g], crs[:, q, g:g + 1],
                                                              x2b[:, g], ALU.mult, ALU.add)
                    last.then_inc(S["x3_done"], 1)
                if mid:
                    dve.wait_ge(S["x3_done"], k + 2)
                    stats(x3[:, (s + 1) % 4], st3, mv3, S["st3_done"], S["mv3_done"], k + 2)
                    nc.vector.tensor_scalar(pin3[:], mv3[:, :, 1], LN_EPS, None, ALU.add).then_inc(S["pin3_done"], 1)
                if conv:
                    dve.wait_ge(S["xn_hi_done"], k + 1)
                    nc.vector.tensor_tensor(xn_lo[:], GI[:], xn_hi[:].bitcast(f32), ALU.subtract).then_inc(S["xn_lo_done"], 1)
                if mid:
                    dve.wait_ge(S["rs3_done"], k + 2)
                    wait(dve, S["xh3_done"], k + 1)
                    nc.vector.scalar_tensor_tensor(nm3[:], mv3[:, :, 0], -1.0, rs3[:], ALU.mult,
                                                   ALU.mult).then_inc(S["nm3_done"], 1)
                if gcn:
                    dve.wait_ge(S["w1_done"], k + 3)
                    wait(dve, S["a1_done"], k + 2)
                    nc.vector.tensor_tensor(y1[:], XA[:], s_in[:, p].unsqueeze(2).broadcast_to([P, G, P]),
                                            ALU.mult).then_inc(S["y1_done"], 1)
                if gate:
                    dve.wait_ge(S["ot_psum"], k)
                    if not isinstance(k, int) or u - 1 + p > 0:
                        dve.wait_ge(x_stored[q], (u - 1 + p) * 16)
                    nc.vector.tensor_tensor(x4[:, q], XB[:], x3[:, (s + 3) % 4], ALU.add).then_inc(S["x4_done"], 1)
                if gcn:
                    dve.wait_ge(S["a1_done"], k + 3)
                    dve.wait_ge(S["self1_done"], k + 3)
                    dve.wait_ge(S["ns_done"], k + 3)
                    wait(dve, S["spa_done"], k + 2)
                    for g in range(G):
                        last = nc.vector.scalar_tensor_tensor(pre[:, g], XC[:, g], ns_out[:, g:g + 1], self1[:, g],
                                                              ALU.mult, ALU.add)
                    last.then_inc(S["pre_done"], 1)

            steps(dve, body)

        @block.tensor
        def _(pe):
            def transposes(dst, src):
                for g in range(G):
                    last = nc.tensor.transpose(dst[:, g], src[:, g], ident[:])
                return last

            def per_graph(dst, lhs, rhs):
                for g in range(G):
                    last = nc.tensor.matmul(dst[:, g], lhs(g), rhs(g), start=True, stop=True)
                return last

            def split_product(dst, w, hi, lo, start, stop):
                nc.tensor.matmul(dst, w_hi[:, w], hi, start=start, stop=False)
                nc.tensor.matmul(dst, w_hi[:, w], lo, start=False, stop=False)
                return nc.tensor.matmul(dst, w_lo[:, w], hi, start=False, stop=stop)

            def taps(lo_tap, hi_tap):
                for t in range(lo_tap, hi_tap):
                    last = split_product(CB[:], W_CONV2 + t, c1_hi[:, :, t:t + P], c1_lo[:, :, t:t + P],
                                         t == 0, t == TAPS - 1)
                return last

            def body(k, u, s, prep, gcn, mid, conv, gate):
                p, q = s % 2, (s + 1) % 2
                if isinstance(k, int) and k == -2:
                    pe.wait_ge(S["ident_made"], 1)
                    pe.wait_ge(S["loads_consts"], 9 * 16)
                    pe.wait_ge(S["w1_sum"], 1)
                if isinstance(k, int) and k == 0:
                    pe.wait_ge(S["weights_split"], 1)
                    pe.wait_ge(S["bm3_made"], 1)
                if conv:
                    pe.wait_ge(S["xh3_done"], k + 1)
                    wait(pe, S["y1_done"], k + 2)
                    transposes(XA, xh3).then_inc(S["ht_psum"], 1)
                if gate:
                    wait(pe, S["z2t_done"], k + 1)
                    wait(pe, S["t0_done"], k + 2)
                    wait(pe, S["self1_done"], k + 2)
                    hi, lo = ht_hi[:, q], ht_lo[:, q]
                    split_product(GR[:], W_HH, hi, lo, True, False)
                    split_product(GZ[:], W_HH + 1, hi, lo, True, False)
                    split_product(GH[:], W_HH + 2, hi, lo, True, True).then_inc(S["gate_h_done"], 1)
                    pe.wait_ge(S["xn_lo_done"], k)
                    for i, dst in enumerate((GR, GZ, GI)):
                        split_product(dst[:], W_IH + 3 + i, xn_hi[:], xn_lo[:], i == 2, False)
                if gcn:
                    pe.wait_ge(S["xh0_done"], k + 3)
                    wait(pe, S["ht_hi_done"], k + 1)
                    wait(pe, S["y1_done"], k + 2)
                    transposes(XA, xh0).then_inc(S["h0t_psum"], 1)
                if conv:
                    pe.wait_ge(S["ht_lo_done"], k + 1)
                    wait(pe, S["cv_done"], k)
                    split_product(CB[:], W_CONV1, ht_hi[:, p], ht_lo[:, p], True, True).then_inc(S["conv1_done"], 1)
                    wait(pe, S["x4_done"], k - 1)
                    split_product(XB[:], W_SE, ht_hi[:, p], ht_lo[:, p], True, True).then_inc(S["se_done"], 1)
                if gate:
                    pe.wait_ge(S["xc_lo_done"], k)
                    for i, dst in enumerate((GR, GZ, GI)):
                        last = split_product(dst[:], W_IH + i, xc_hi[:], xc_lo[:], False, True)
                    last.then_inc(S["gates_done"], 1)
                if gcn:
                    pe.wait_ge(S["h0t_done"], k + 3)
                    per_graph(XA, lambda g: h0t[:, g], lambda g: w0[:]).then_inc(S["w0_done"], 1)
                if conv:
                    pe.wait_ge(S["c1_lo_done"], k + 1)
                    taps(0, 1)
                if gcn:
                    pe.wait_ge(adj_loaded[p], (u + 2) * 16)
                    wait(pe, S["gez_done"], k)
                    wait(pe, S["t0_done"], k + 2)
                    transposes(GZ, adj_in[:, p]).then_inc(S["adj_t_psum"], 1)
                if conv:
                    wait(pe, S["ge_done"], k)
                    nc.tensor.matmul(GR[:], ones[:], bm3[:], start=True, stop=True, skip_group_check=True)
                    for g in range(G):
                        last = nc.tensor.matmul(GR[:, g], ht[:, p, g], w_raw[:, W_MSG], start=False, stop=True,
                                                skip_group_check=True)
                    last.then_inc(S["msg_psum"], 1)
                if gcn:
                    pe.wait_ge(S["y0_done"], k + 3)
                    pe.wait_ge(S["adj_t_done"], k + 3)
                    per_graph(GZ, lambda g: adj_t[:, (s + 2) % 4, g], lambda g: y0[:, g]).then_inc(S["a0_done"], 1)
                if conv:
                    taps(1, 4)
                    for name in ("dl_s", "dr_s", "dl_q", "dr_q"):
                        pe.wait_ge(S[name], k + 1)
                    per_graph(XB, lambda g: dl[:, g], lambda g: dr[:, g]).then_inc(S["dist_done"], 1)
                    taps(4, 6)
                if mid:
                    pe.wait_ge(S["h2_done"], k + 2)
                    wait(pe, S["msg_done"], k + 1)
                    wait(pe, S["z2t_done"], k + 1)
                    per_graph(GR, lambda g: h2[:, g], lambda g: adj_t[:, (s + 1) % 4, g]).then_inc(S["a2_done"], 1)
                if conv:
                    taps(6, 8)
                if mid:
                    pe.wait_ge(S["z2t_done"], k + 2)
                    wait(pe, S["pre_done"], k + 2)
                    per_graph(XC, lambda g: z2t[:, g], lambda g: w2_sb[:]).then_inc(S["w2_done"], 1)
                if conv:
                    pe.wait_ge(S["m3_done"], k + 1)
                    pe.wait_ge(S["msg_done"], k + 1)
                    wait(pe, S["vn_done"], k)
                    per_graph(GI, lambda g: msg[:, g], lambda g: m3[:, g]).then_inc(S["a3_done"], 1)
                    taps(8, 12)
                if gcn:
                    pe.wait_ge(S["z1_done"], k + 3)
                    pe.wait_ge(S["z1b_done"], k + 3)
                    transposes(XA, z1).then_inc(S["z1t_psum"], 1)
                if conv:
                    taps(12, 14)
                if gcn:
                    pe.wait_ge(S["z1t_done"], k + 3)
                    wait(pe, S["rn_done"], k)
                    wait(pe, S["self1_done"], k + 2)
                    per_graph(XA, lambda g: z1t[:, g], lambda g: w1n[:])
                    per_graph(GH, lambda g: z1t[:, g], lambda g: w1ns[:]).then_inc(S["w1_done"], 1)
                if gate:
                    pe.wait_ge(S["ot_done"], k)
                    wait(pe, S["ex_done"], k + 1)
                    wait(pe, S["x4_done"], k - 1)
                    transposes(XB, ot).then_inc(S["ot_psum"], 1)
                if conv:
                    taps(14, 15)
                if gcn:
                    pe.wait_ge(S["y1_done"], k + 3)
                    wait(pe, S["x3_done"], k + 2)
                    wait(pe, S["pre_done"], k + 2)
                    per_graph(XC, lambda g: adj_t[:, (s + 2) % 4, g], lambda g: y1[:, g]).then_inc(S["a1_done"], 1)
                if conv:
                    taps(15, TAPS).then_inc(S["conv2_done"], 1)

            steps(pe, body)


def kernel(**inputs):
    import numpy as np
    import concourse.bacc as bacc
    from concourse.bass_utils import run_bass_kernel_spmd

    a = {n: np.asarray(v) for n, v in inputs.items()}
    w3 = {n[len("L3_gnn_"):]: v for n, v in a.items() if n.startswith("L3_gnn_")}
    b_ih, b_hh = w3["b_ih"].reshape(3, P), w3["b_hh"].reshape(3, P)
    vecs = np.stack([a["L1_gnn_gamma"], a["L1_gnn_beta"],
                     w3["bn1_g"], w3["bn1_b"], w3["bn1_m"], w3["bn1_v"],
                     w3["bn2_g"], w3["bn2_b"], w3["bn2_m"], w3["bn2_v"],
                     b_ih[0], b_ih[1], b_ih[2], b_hh[0], b_hh[1], b_hh[2]], axis=1)
    arrays = {
        "x": a["x"], "adj": a["adj"], "mask_t": a["nodemask"].T,
        "w0_t": a["L0_gnn_W"].T, "w1_self": a["L1_gnn_W_self"], "w1_neigh": a["L1_gnn_W_neigh"],
        "w2": a["L2_gnn_weight"],
        "conv2_t": w3["conv2_w"].transpose(1, 2, 0),
        "conv1_t": w3["conv1_w"][:, :, 0].T, "msg_t": w3["w_msg"].T, "se_t": w3["w_se"].T,
        "ih_t": w3["w_ih"].reshape(3, P, 2, P).transpose(3, 2, 0, 1).reshape(P, 6, P),
        "hh_t": w3["w_hh"].reshape(3, P, P).transpose(2, 0, 1),
        "vecs": vecs, "b_se": w3["b_se"].reshape(3, 1),
        "rows": np.stack([a["L0_gnn_b"], a["L2_gnn_bias"], w3["b_msg"]]),
    }
    arrays = {n: np.ascontiguousarray(v) for n, v in arrays.items()}
    nc = bacc.Bacc("TRN2", target_bir_lowering=False, num_devices=1)
    args = [nc.dram_tensor(f"in_{n}", v.shape, mybir.dt.from_np(v.dtype), kind="ExternalInput").ap()
            for n, v in arrays.items()]
    args.append(nc.dram_tensor("out_0", (GRAPHS, P, P), mybir.dt.float32, kind="ExternalOutput").ap())
    graph_net(nc, *args)
    r = run_bass_kernel_spmd(nc, [{f"in_{n}": v for n, v in arrays.items()}], core_ids=[0])
    return r.results[0]["out_0"]
```

```python
import concourse.bass as bass
from concourse import mybir
from contextlib import ExitStack


P = 128
GRAPHS = 128
G = 4
NG = GRAPHS // G
GP = G * P
TAPS = 17
PAD = TAPS // 2
HALF = P // 2
E_TAPS, O_TAPS = (TAPS + 1) // 2, TAPS // 2
HROW = HALF + PAD + 2
SROW = HALF + PAD
LN_EPS = 1e-5
EXP_LN_TABLES = 6
DEG_EPS = 1e-8

W_CONV2, W_CONV1, W_MSG, W_SE, W_IH, W_HH = 0, TAPS, TAPS + 1, TAPS + 2, TAPS + 3, TAPS + 9
W_SUM = TAPS + 12
NW = W_SUM + O_TAPS

VECS = ["gamma", "beta", "bn1_g", "bn1_b", "bn1_m", "bn1_v", "bn2_g", "bn2_b", "bn2_m", "bn2_v",
        "b_ih_r", "b_ih_z", "b_ih_n", "b_hh_r", "b_hh_z", "b_hh_n"]


def graph_net(nc, x, adj, mask_t, w0_t, w1_self, w1_neigh, w2, conv2_t, conv1_t, msg_t, se_t, ih_t,
              hh_t, vecs, b_se, rows, out):
    f32, f32r, bf16 = mybir.dt.float32, mybir.dt.float32r, mybir.dt.bfloat16
    ALU = mybir.AluOpType
    ACT = mybir.ActivationFunctionType
    AX = mybir.AxisListType

    x_g = x.rearrange("(s g) n f -> s n g f", g=G)
    adj_g = adj.rearrange("(s g) n m -> s n g m", g=G)
    out_g = out.rearrange("(s g) n f -> s n g f", g=G)

    with ExitStack() as ctx:
        def sb(name, shape, dt=f32):
            return ctx.enter_context(nc.sbuf_tensor(name, shape, dt))

        w_raw = sb("w_raw", [P, NW, P])
        w_hi = sb("w_hi", [P, NW, P], f32r)
        w_lo = sb("w_lo", [P, NW, P], f32r)
        w0 = sb("w0", [P, P])
        w1n = sb("w1n", [P, P])
        w1s = sb("w1s", [P, P])
        w1ns = sb("w1ns", [P, P])
        w2_sb = sb("w2_sb", [P, P])
        ident = sb("ident", [P, P])
        vec = sb("vec", [P, len(VECS)])
        bnp = sb("bnp", [P, 2])
        neg_half = sb("neg_half", [P, 8])
        bns = sb("bns", [P, 2])
        bnr = sb("bnr", [P, 2])
        bns_n = sb("bns_n", [P, 1])
        bnb = sb("bnb", [P, 2])
        gb = sb("gb", [P, 4])
        bse = sb("bse", [P, 1])
        b0_bc = sb("b0_bc", [P, P])
        b2_bc = sb("b2_bc", [P, P])
        bm_f = sb("bm_f", [P, P])
        bm_r = sb("bm_r", [P, P])
        bm3 = sb("bm3", [96, G, P], bf16)
        ones = sb("ones", [96, P], bf16)
        mask_sb = sb("mask_sb", [P, GRAPHS])

        x_in = sb("x_in", [P, 2, G, P])
        adj_in = sb("adj_in", [P, 2, G, P])
        adj_t = sb("adj_t", [P, 4, G, P])
        st0 = sb("st0", [P, G, 6])
        mv0 = sb("mv0", [P, G, 2])
        deg = sb("deg", [P, G])
        deg0 = sb("deg0", [P, G])
        pin0 = sb("pin0", [P, G])
        rs0 = sb("rs0", [P, G])
        pind = sb("pind", [P, 8])
        rsd = sb("rsd", [P, 8])
        r0d = sb("r0d", [P, G])
        nm0 = sb("nm0", [P, G])
        dm = sb("dm", [P, G])
        s_in = sb("s_in", [P, 2, G])
        cin = sb("cin", [P, 8])
        cs0 = sb("cs0", [P, G])
        crs = sb("crs", [P, 2, 8])
        ns_out = sb("ns_out", [P, G])
        xh0 = sb("xh0", [P, G, P])
        h0t = sb("h0t", [P, G, P])
        y0 = sb("y0", [P, G, P])
        t0 = sb("t0", [P, G, P])
        u0 = sb("u0", [P, G, P])
        x1 = sb("x1", [P, G, P])

        st1 = sb("st1", [P, G, 6])
        mv1 = sb("mv1", [P, G, 2])
        e1 = sb("e1", [P, G])
        cc = sb("cc", [P, G, P])
        stc = sb("stc", [P, G, 6])
        mvc = sb("mvc", [P, G, 2])
        pin1 = sb("pin1", [P, G])
        q1 = sb("q1", [P, G])
        nmq = sb("nmq", [P, G])
        z1 = sb("z1", [P, G, P])
        z1t = sb("z1t", [P, G, P])
        y1 = sb("y1", [P, G, P])
        self1 = sb("self1", [P, G, P])
        pre = sb("pre", [P, G, P])
        sp_a = sb("sp_a", [P, G, P])
        sp_l = sb("sp_l", [P, G, P])
        sp = sb("sp", [P, G, P])
        x2 = sb("x2", [P, G, P])
        x2b = sb("x2b", [P, G, P])
        st2 = sb("st2", [P, G, 6])
        mv2 = sb("mv2", [P, G, 2])
        pin2 = sb("pin2", [P, G])
        rs2 = sb("rs2", [P, G])
        r2d = sb("r2d", [P, G])
        h2 = sb("h2", [P, G, P])
        nm2 = sb("nm2", [P, G])
        z2t = sb("z2t", [P, G, P])
        x3 = sb("x3", [P, 4, G, P])
        st3 = sb("st3", [P, G, 6])
        mv3 = sb("mv3", [P, G, 2])
        pin3 = sb("pin3", [P, G])
        rs3 = sb("rs3", [P, G])
        nm3 = sb("nm3", [P, G])
        xh3 = sb("xh3", [P, G, P])

        ht = sb("ht", [P, 2, G, P])
        ht_hi = sb("ht_hi", [P, 2, G, P], f32r)
        ht_lo = sb("ht_lo", [P, 2, G, P], f32r)
        htb = sb("htb", [P, G, P])
        c1 = sb("c1", [P, G, 2, HROW])
        c1_hi = sb("c1_hi", [P, G, 2, HROW], f32r)
        c1_lo = sb("c1_lo", [P, G, 2, HROW], f32r)
        cs = sb("cs", [P, G, SROW])
        cs_hi = sb("cs_hi", [P, G, SROW], f32r)
        cs_lo = sb("cs_lo", [P, G, SROW], f32r)
        pe_sb = sb("pe_sb", [P, G, HALF + 2])
        he = sb("he", [P, G, HALF])
        ho = sb("ho", [P, G, HALF])
        msg = sb("msg", [P, G, P])
        dl = sb("dl", [96, G, P])
        dr = sb("dr", [96, G, P])
        ex = sb("ex", [P, G, P])
        m3 = sb("m3", [P, G, P])
        xn_hi = sb("xn_hi", [P, G, P], f32r)
        xn_lo = sb("xn_lo", [P, G, P], f32r)

        cv = sb("cv", [P, G, P])
        xc_hi = sb("xc_hi", [P, G, P], f32r)
        xc_lo = sb("xc_lo", [P, G, P], f32r)
        ge = sb("ge", [P, 2, GP])
        rz = sb("rz", [P, 2, GP])
        rn = sb("rn", [P, GP])
        vn = sb("vn", [P, GP])
        ne = sb("ne", [P, GP])
        nq = sb("nq", [P, GP])
        nn = sb("nn", [P, GP])
        hd = sb("hd", [P, GP])
        zd = sb("zd", [P, GP])
        ot = sb("ot", [P, G, P])
        x4 = sb("x4", [P, 2, G, P])

        def bank(name):
            return ctx.enter_context(nc.psum_tensor(name, [P, G, P], f32))

        CB = bank("bank_conv")
        GR, GZ, GI, GH = bank("bank_r"), bank("bank_z"), bank("bank_in"), bank("bank_hn")
        XA, XB, XC = bank("bank_a"), bank("bank_b"), bank("bank_c")

        def flat(t):
            return t.rearrange("p g n -> p (g n)")

        cb = flat(CB)
        CP = cb[:, 0:G * (HALF + 2)].rearrange("p (g i) -> p g i", g=G)
        CR = cb[:, 0:G * HALF].rearrange("p (g i) -> p g i", g=G)
        CQ = cb[:, G * HALF:GP].rearrange("p (g i) -> p g i", g=G)

        def parity(t, i):
            return t.rearrange("p g (i two) -> p g i two", two=2)[:, :, :, i]

        names = """
            loads_weights loads_consts ident_zero ident_made halves_set bn_in bn_pow bn_scale bn_shift
            weights_hi weights_split se_zero gate_bias pads_set bm_hi bm_r1 bm_mid bm_r2 bm3_made w1_sum
            x_loaded_0 x_loaded_1 adj_loaded_0 adj_loaded_1 x_stored_0 x_stored_1
            st0_done mv0_done deg_done deg0_done pin0_done rs0_done pind_done rsd_done r0d_done nm0_done dm_done xh0_done
            adj_t_psum adj_t_done h0t_psum h0t_done cs0_done is0_done cin_done crs_done ns_done
            w0_done y0_done a0_done t0_done u0_done x1_done
            st1_done mv1_done e1_done c_done stc_done mvc_done pin1_done q1_done nmq_done z1_done z1b_done
            z1t_psum z1t_done w1_done y1_done self1_done a1_done pre_done spa_done spe_done spl_done
            sp_done x2_done x2b_done st2_done mv2_done pin2_done rs2_done r2d_done nm2_done h2_done
            a2_done z2t_done w2_done x3_done st3_done mv3_done pin3_done rs3_done nm3_done
            xh3_done
            ht_psum ht_done ht_hi_done ht_lo_done htb_done conv1_done c1_done c1_hi_done c1_lo_done
            cs_done cs_hi_done cs_lo_done convp_done pe_done he_done ho_done  hq_done w_sum_made
            se_done dl_s dr_s dl_q dr_q msg_psum msg_done dist_done ex_done m3_done
            a3_done xn_hi_done xn_lo_done conv2_done
            cv_done xc_hi_done xc_lo_done gate_h_done gates_done w1n_done gez_done ge_done gl_done rz_done rn_done vn_done
            ne_done nl_done nq_done nn_done hd_done zd_done ot_done ot_psum x4_done
            tick_dve tick_sp
        """.split()
        S = {n: ctx.enter_context(nc.semaphore(n)) for n in names}

        x_loaded, adj_loaded = (S["x_loaded_0"], S["x_loaded_1"]), (S["adj_loaded_0"], S["adj_loaded_1"])
        x_stored = (S["x_stored_0"], S["x_stored_1"])

        def wait(eng, sem, n):
            if not isinstance(n, int):
                eng.wait_ge(sem, n)
            elif n > 0:
                eng.wait_ge(sem, min(n, NG))

        def steps(eng, body):
            def peeled(k):
                body(k, k // 2, k % 4, *(0 <= k + ahead < NG for ahead in (3, 2, 1, 0, -1)))

            for k in range(-3, 4):
                peeled(k)
            with eng.Fori(1, NG // 4 - 1) as j:
                for s in range(4):
                    body(j * 4 + s, j * 2 + s // 2, s, True, True, True, True, True)
            for k in range(NG - 4, NG + 1):
                peeled(k)

        block = ctx.enter_context(nc.Block())

        @block.sync
        def _(sp):
            def load_constants():
                n_w = 0
                for dst, src in ((w0[:], w0_t), (w1n[:], w1_neigh), (w1s[:], w1_self), (w2_sb[:], w2),
                                 (vec[:], vecs), (mask_sb[:], mask_t),
                                 (b0_bc[:], rows[0:1, :].broadcast_to([P, P])),
                                 (b2_bc[:], rows[1:2, :].broadcast_to([P, P])),
                                 (bm_f[:], rows[2:3, :].broadcast_to([P, P]))):
                    sp.dma_start(dst, src).then_inc(S["loads_consts"], 16)
                    n_w += 1
                assert n_w == 9

            def load(g, slot):
                wait(sp, S["x1_done"], g - 1)
                sp.sem_inc(S["tick_sp"], 1)
                sp.dma_start(x_in[:, slot], x_g[g]).then_inc(x_loaded[slot], 16)
                wait(sp, S["deg_done"], g - 1)
                sp.sem_inc(S["tick_sp"], 1)
                wait(sp, S["adj_t_psum"], g - 1)
                sp.sem_inc(S["tick_sp"], 1)
                sp.dma_start(adj_in[:, slot], adj_g[g]).then_inc(adj_loaded[slot], 16)

            def load_weights():
                sp.wait_ge(S["se_zero"], 2)
                sp.dma_start(w_raw[:, W_CONV2:W_CONV2 + TAPS, :], conv2_t).then_inc(S["loads_weights"], 16)
                sp.dma_start(w_raw[:, W_CONV1, :], conv1_t).then_inc(S["loads_weights"], 16)
                sp.dma_start(w_raw[:, W_MSG, :], msg_t).then_inc(S["loads_weights"], 16)
                sp.dma_start(w_raw[:, W_IH:W_IH + 6, :], ih_t).then_inc(S["loads_weights"], 16)
                sp.dma_start(w_raw[:, W_HH:W_HH + 3, :], hh_t).then_inc(S["loads_weights"], 16)
                for r in range(3):
                    sp.dma_start(w_raw[:, W_SE, 32 * r:32 * r + 3], se_t).then_inc(S["loads_weights"], 16)
                    sp.dma_start(bse[32 * r:32 * r + 3, 0:1], b_se).then_inc(S["loads_weights"], 16)

            def body(k, u, s, prep, gcn, mid, conv, gate):
                if isinstance(k, int) and k == -3:
                    load(0, 0)
                    load_constants()
                if not isinstance(k, int) or k + 4 < NG:
                    load(k + 4, s % 2)
                if isinstance(k, int) and k == -3:
                    load_weights()
                if gate:
                    wait(sp, S["x4_done"], k)
                    sp.sem_inc(S["tick_sp"], 1)
                    sp.dma_start(out_g[k - 1], x4[:, (s + 1) % 2]).then_inc(x_stored[(s + 1) % 2], 16)

            steps(sp, body)
            sp.wait_ge(S["x_stored_0"], 16 * NG // 2)
            sp.wait_ge(S["x_stored_1"], 16 * NG // 2)

        @block.gpsimd
        def _(pool):
            nc.gpsimd.memset(w_raw[:, W_SE, :], 0.0).then_inc(S["se_zero"], 1)
            nc.gpsimd.memset(bse[:], 0.0).then_inc(S["se_zero"], 1)
            nc.gpsimd.memset(neg_half[:], -0.5).then_inc(S["halves_set"], 1)
            nc.gpsimd.memset(ident[:], 0.0).then_inc(S["ident_zero"], 1)
            pool.wait_ge(S["ident_zero"], 1)
            nc.gpsimd.affine_select(out=ident[:], in_=ident[:], compare_op=ALU.not_equal, fill=1.0, base=0,
                                    pattern=[[-1, P]], channel_multiplier=1).then_inc(S["ident_made"], 1)
            pool.wait_ge(S["halves_set"], 1)

            def constants():
                pool.wait_ge(S["bn_in"], 1)
                nc.gpsimd.tensor_tensor(bnr[:], bnp[:], neg_half[:, 0:2], ALU.pow).then_inc(S["bn_pow"], 1)
                nc.gpsimd.memset(c1[:], 0.0).then_inc(S["pads_set"], 1)
                nc.gpsimd.memset(c1_hi[:].bitcast(f32), 0.0).then_inc(S["pads_set"], 1)
                nc.gpsimd.memset(c1_lo[:].bitcast(f32), 0.0).then_inc(S["pads_set"], 1)

            def body(k, u, s, prep, gcn, mid, conv, gate):
                p, q = s % 2, (s + 1) % 2
                if isinstance(k, int) and k == -2:
                    constants()
                if conv:
                    wait(pool, S["ht_done"], k + 1)
                    wait(pool, S["bn_shift"], 1)
                    wait(pool, S["ho_done"], k)
                    nc.gpsimd.tensor_tensor(htb[:], ht[:, p], bnb[:, 1:2].unsqueeze(2).broadcast_to([P, G, P]),
                                            ALU.add).then_inc(S["htb_done"], 1)
                if mid:
                    wait(pool, S["pin2_done"], k + 2)
                    nc.gpsimd.tensor_tensor(rs2[:], pin2[:], neg_half[:, 0:G], ALU.pow).then_inc(S["rs2_done"], 1)
                    wait(pool, S["loads_consts"], 9 * 16)
                    wait(pool, S["x2_done"], k + 2)
                    wait(pool, S["x3_done"], k + 1)
                    nc.gpsimd.tensor_tensor(x2b[:], x2[:], b2_bc[:].unsqueeze(1).broadcast_to([P, G, P]),
                                            ALU.add).then_inc(S["x2b_done"], 1)
                if gcn:
                    wait(pool, S["cin_done"], k + 3)
                    wait(pool, S["x3_done"], k + 1)
                    nc.gpsimd.tensor_tensor(crs[:, p], cin[:], neg_half[:, 0:8], ALU.pow).then_inc(S["crs_done"], 1)
                if prep:
                    wait(pool, S["pind_done"], k + 4)
                    wait(pool, S["dm_done"], k + 3)
                    wait(pool, S["y0_done"], k + 3)
                    nc.gpsimd.tensor_tensor(rsd[:], pind[:], neg_half[:], ALU.pow).then_inc(S["rsd_done"], 1)
                if conv:
                    wait(pool, S["pe_done"], k + 1)
                    wait(pool, S["htb_done"], k + 1)
                    wait(pool, S["cv_done"], k)
                    nc.gpsimd.tensor_tensor(he[:], parity(htb, 0), pe_sb[:, :, 0:HALF], ALU.add).then_inc(S["he_done"], 1)
                    nc.gpsimd.tensor_tensor(ho[:], parity(htb, 1), pe_sb[:, :, 1:HALF + 1],
                                            ALU.subtract).then_inc(S["ho_done"], 1)
                    wait(pool, S["ex_done"], k + 1)
                    wait(pool, S["adj_t_done"], k + 1)
                    wait(pool, S["a3_done"], k)
                    nc.gpsimd.tensor_tensor(m3[:], ex[:], adj_t[:, s], ALU.mult).then_inc(S["m3_done"], 1)
                if gcn:
                    wait(pool, S["pin1_done"], k + 3)
                    wait(pool, S["z1_done"], k + 2)
                    wait(pool, S["z1b_done"], k + 2)
                    nc.gpsimd.tensor_tensor(q1[:], pin1[:], neg_half[:, 0:G], ALU.pow).then_inc(S["q1_done"], 1)
                if gate:
                    wait(pool, S["nn_done"], k)
                    wait(pool, S["ht_done"], k)
                    nc.gpsimd.tensor_tensor(hd[:], flat(ht[:, q]), nn[:], ALU.subtract).then_inc(S["hd_done"], 1)
                    wait(pool, S["rz_done"], k)
                    wait(pool, S["hd_done"], k)
                    nc.gpsimd.tensor_tensor(zd[:], hd[:], rz[:, 1], ALU.mult).then_inc(S["zd_done"], 1)
                if prep:
                    wait(pool, S["pin0_done"], k + 4)
                    wait(pool, S["r0d_done"], k + 3)
                    nc.gpsimd.tensor_tensor(rs0[:], pin0[:], neg_half[:, 0:G], ALU.pow).then_inc(S["rs0_done"], 1)
                if mid:
                    wait(pool, S["pin3_done"], k + 2)
                    wait(pool, S["xh3_done"], k + 1)
                    nc.gpsimd.tensor_tensor(rs3[:], pin3[:], neg_half[:, 0:G], ALU.pow).then_inc(S["rs3_done"], 1)
                if gate:
                    wait(pool, S["zd_done"], k)
                    wait(pool, S["ot_psum"], k - 1)
                    nc.gpsimd.tensor_tensor(flat(ot[:]), zd[:], nn[:], ALU.add).then_inc(S["ot_done"], 1)

            steps(pool, body)

        @block.scalar
        def _(act):
            nc.scalar.add_instruction(mybir.InstLoadActFuncSet(
                name=nc.get_next_instruction_name(), engine=mybir.EngineType.Activation, act_func_set_id=EXP_LN_TABLES))

            def scaled(dst, src, scale, shift, sem, func=ACT.Identity, graphs=G):
                for g in range(graphs):
                    last = nc.scalar.activation(dst[:, g], src[:, g], func, bias=shift[:, g:g + 1],
                                                scale=scale[:, g:g + 1])
                last.then_inc(sem, 1)

            def body(k, u, s, prep, gcn, mid, conv, gate):
                p, q = s % 2, (s + 1) % 2
                if mid:
                    act.wait_ge(S["pre_done"], k + 2)
                    nc.scalar.activation(sp_a[:], pre[:], ACT.Abs).then_inc(S["spa_done"], 1)
                if conv:
                    act.wait_ge(S["ht_psum"], k + 1)
                    wait(act, S["hd_done"], k - 1)
                    nc.scalar.activation(ht[:, p], XA[:], ACT.Relu).then_inc(S["ht_done"], 1)
                    wait(act, S["gate_h_done"], k - 1)
                    nc.scalar.activation(ht_hi[:, p], XA[:], ACT.Relu).then_inc(S["ht_hi_done"], 1)
                if gate:
                    act.wait_ge(S["cv_done"], k)
                    wait(act, S["gates_done"], k - 1)
                    nc.scalar.activation(xc_hi[:], cv[:], ACT.Relu).then_inc(S["xc_hi_done"], 1)
                if mid:
                    act.wait_ge(S["spa_done"], k + 2)
                    nc.scalar.activation(sp_a[:], sp_a[:], ACT.Exp, scale=-1.0).then_inc(S["spe_done"], 1)
                    act.wait_ge(S["spe_done"], k + 2)
                    wait(act, S["sp_done"], k + 1)
                    nc.scalar.activation(sp_l[:], sp_a[:], ACT.Ln, bias=1.0).then_inc(S["spl_done"], 1)
                if gcn:
                    act.wait_ge(S["h0t_psum"], k + 3)
                    wait(act, S["w0_done"], k + 2)
                    nc.scalar.activation(h0t[:], XA[:], ACT.Relu).then_inc(S["h0t_done"], 1)
                    act.wait_ge(S["adj_t_psum"], k + 3)
                    wait(act, S["m3_done"], k - 1)
                    wait(act, S["crs_done"], k + 2)
                    for g in range(G):
                        last = nc.scalar.activation(adj_t[:, (s + 2) % 4, g], XC[:, g], ACT.Copy,
                                                    accum_out=cin[:, g:g + 1])
                    last.then_inc(S["adj_t_done"], 1)
                if isinstance(k, int) and k == -2:
                    act.wait_ge(S["w_sum_made"], 1)
                    nc.scalar.activation(w_hi[:], w_raw[:], ACT.Copy).then_inc(S["weights_hi"], 1)
                if conv:
                    act.wait_ge(S["conv1_done"], k + 1)
                    act.wait_ge(S["bn_shift"], 1)
                    act.wait_ge(S["pads_set"], 6)
                    wait(act, S["c1_lo_done"], k)
                    wait(act, S["cs_done"], k)
                    inner = slice(PAD // 2, PAD // 2 + HALF)
                    by_parity = CB.rearrange("p g (i two) -> p g two i", two=2)
                    nc.scalar.activation(c1[:, :, :, inner], by_parity, ACT.Relu, bias=bnb[:, 0:1],
                                         scale=bns[:, 0:1]).then_inc(S["c1_done"], 1)
                    wait(act, S["conv2_done"], k)
                    nc.scalar.activation(c1_hi[:, :, :, inner], by_parity, ACT.Relu, bias=bnb[:, 0:1],
                                         scale=bns[:, 0:1]).then_inc(S["c1_hi_done"], 1)
                    act.wait_ge(S["se_done"], k + 1)
                    act.wait_ge(S["loads_weights"], 11 * 16)
                    wait(act, S["dist_done"], k)
                    nc.scalar.activation(dl[0:32], XB[0:32], ACT.Identity, bias=bse[0:32, 0:1]).then_inc(S["dl_s"], 1)
                    nc.scalar.activation(dl[32:64], XB[32:64], ACT.Square, bias=bse[32:64, 0:1]).then_inc(S["dl_q"], 1)
                if gate:
                    act.wait_ge(S["gates_done"], k)
                    act.wait_ge(S["gate_bias"], 3)
                    wait(act, S["rz_done"], k - 1)
                    nc.scalar.activation(ge[:, 1], flat(GZ[:]), ACT.Exp, bias=gb[:, 1:2],
                                         scale=-1.0).then_inc(S["gez_done"], 1)
                    nc.scalar.activation(ge[:, 0], flat(GR[:]), ACT.Exp, bias=gb[:, 0:1],
                                         scale=-1.0).then_inc(S["ge_done"], 1)
                if conv:
                    wait(act, S["dist_done"], k)
                    nc.scalar.activation(dr[64:96], XB[64:96], ACT.Square, bias=bse[64:96, 0:1]).then_inc(S["dr_q"], 1)
                if gate:
                    act.wait_ge(S["ge_done"], k)
                    nc.scalar.activation(ge[:], ge[:], ACT.Ln, bias=1.0).then_inc(S["gl_done"], 1)
                if mid:
                    act.wait_ge(S["nm2_done"], k + 2)
                    wait(act, S["a2_done"], k + 1)
                    scaled(h2, x2, r2d, nm2, S["h2_done"], ACT.Relu)
                if conv:
                    act.wait_ge(S["msg_psum"], k + 1)
                    wait(act, S["a3_done"], k)
                    nc.scalar.activation(msg[:], GR[:], ACT.Relu).then_inc(S["msg_done"], 1)
                if gate:
                    act.wait_ge(S["gl_done"], k)
                    wait(act, S["rn_done"], k - 1)
                    wait(act, S["zd_done"], k - 1)
                    nc.scalar.activation(rz[:], ge[:], ACT.Exp, scale=-1.0).then_inc(S["rz_done"], 1)
                if conv:
                    act.wait_ge(S["cs_done"], k + 1)
                    wait(act, S["conv2_done"], k)
                    nc.scalar.activation(cs_hi[:], cs[:], ACT.Copy).then_inc(S["cs_hi_done"], 1)
                    act.wait_ge(S["convp_done"], k + 1)
                    wait(act, S["ho_done"], k)
                    nc.scalar.activation(pe_sb[:], CP, ACT.Copy, scale=bns[:, 1:2]).then_inc(S["pe_done"], 1)
                    act.wait_ge(S["dist_done"], k + 1)
                    wait(act, S["m3_done"], k)
                    nc.scalar.activation(ex[:], XB[:], ACT.Exp).then_inc(S["ex_done"], 1)
                if mid:
                    act.wait_ge(S["a2_done"], k + 2)
                    wait(act, S["w2_done"], k + 1)
                    nc.scalar.activation(z2t[:], GR[:], ACT.Copy).then_inc(S["z2t_done"], 1)
                if gate:
                    act.wait_ge(S["vn_done"], k)
                    wait(act, S["nq_done"], k - 1)
                    nc.scalar.activation(ne[:], vn[:], ACT.Exp, bias=gb[:, 3:4], scale=-2.0).then_inc(S["ne_done"], 1)
                    act.wait_ge(S["ne_done"], k)
                    nc.scalar.activation(ne[:], ne[:], ACT.Ln, bias=1.0).then_inc(S["nl_done"], 1)
                    act.wait_ge(S["nl_done"], k)
                    wait(act, S["nn_done"], k - 1)
                    nc.scalar.activation(nq[:], ne[:], ACT.Exp, scale=-1.0).then_inc(S["nq_done"], 1)
                if gcn:
                    act.wait_ge(S["nmq_done"], k + 3)
                    act.wait_ge(S["q1_done"], k + 3)
                    wait(act, S["z1t_psum"], k + 2)
                    scaled(z1, cc, q1, nmq, S["z1_done"], graphs=G // 2)
                if conv:
                    act.wait_ge(S["a3_done"], k + 1)
                    wait(act, S["gates_done"], k)
                    nc.scalar.activation(xn_hi[:], GI[:], ACT.Copy).then_inc(S["xn_hi_done"], 1)
                if gcn:
                    act.wait_ge(S["z1t_psum"], k + 3)
                    act.wait_ge(S["loads_consts"], 9 * 16)
                    wait(act, S["w1_done"], k + 2)
                    nc.scalar.activation(z1t[:], XA[:], ACT.Identity, bias=vec[:, 1:2],
                                         scale=vec[:, 0:1]).then_inc(S["z1t_done"], 1)
                    act.wait_ge(S["w1_done"], k + 3)
                    wait(act, S["pre_done"], k + 2)
                    nc.scalar.activation(self1[:], GH[:], ACT.Copy).then_inc(S["self1_done"], 1)
                if mid:
                    act.wait_ge(S["nm3_done"], k + 2)
                    wait(act, S["ht_psum"], k + 1)
                    scaled(xh3, x3[:, (s + 1) % 4], rs3, nm3, S["xh3_done"])
                if prep:
                    act.wait_ge(S["nm0_done"], k + 4)
                    act.wait_ge(x_loaded[q], (u + 2 + p) * 16)
                    wait(act, S["h0t_psum"], k + 3)
                    scaled(xh0, x_in[:, q], r0d, nm0, S["xh0_done"])

            steps(act, body)

        @block.vector
        def _(dve):
            nc.vector.memset(dl[64:96], -1.0).then_inc(S["pads_set"], 1)
            nc.vector.memset(dr[32:64], -1.0).then_inc(S["pads_set"], 1)
            nc.vector.memset(ones[:], 1.0 / 32).then_inc(S["pads_set"], 1)
            def constants():
                dve.wait_ge(S["loads_consts"], 9 * 16)
                nc.vector.tensor_tensor(w1ns[:], w1s[:], w1n[:], ALU.add).then_inc(S["w1_sum"], 1)
                for i in range(2):
                    last = nc.vector.tensor_scalar(bnp[:, i:i + 1], vec[:, 5 + 4 * i:6 + 4 * i], LN_EPS, None, ALU.add)
                last.then_inc(S["bn_in"], 1)
                nc.vector.tensor_copy(bm3[:, 0], bm_f[0:96]).then_inc(S["bm_hi"], 1)
                dve.wait_ge(S["bm_hi"], 1)
                nc.vector.tensor_tensor(bm_r[0:96], bm_f[0:96], bm3[:, 0], ALU.subtract).then_inc(S["bm_r1"], 1)
                dve.wait_ge(S["bm_r1"], 1)
                nc.vector.tensor_copy(bm3[32:64, 0], bm_r[32:64])
                nc.vector.tensor_copy(bm3[64:96, 0], bm_r[64:96]).then_inc(S["bm_mid"], 1)
                dve.wait_ge(S["bm_mid"], 1)
                nc.vector.tensor_tensor(bm_f[64:96], bm_r[64:96], bm3[64:96, 0], ALU.subtract).then_inc(S["bm_r2"], 1)
                dve.wait_ge(S["bm_r2"], 1)
                nc.vector.tensor_copy(bm3[64:96, 0], bm_f[64:96]).then_inc(S["bm_mid"], 1)
                dve.wait_ge(S["bm_mid"], 2)
                for g in range(1, G):
                    last = nc.vector.tensor_copy(bm3[:, g], bm3[:, 0])
                last.then_inc(S["bm3_made"], 1)
                nc.vector.tensor_tensor(gb[:, 0:2], vec[:, 10:12], vec[:, 13:15], ALU.add).then_inc(S["gate_bias"], 1)
                dve.wait_ge(S["gate_bias"], 1)
                nc.vector.tensor_scalar(gb[:, 0:2], gb[:, 0:2], -1.0, None, ALU.mult).then_inc(S["gate_bias"], 1)
                nc.vector.tensor_scalar(gb[:, 3:4], vec[:, 12:13], -2.0, None, ALU.mult).then_inc(S["gate_bias"], 1)
                dve.wait_ge(S["bn_pow"], 1)
                for i in range(2):
                    last = nc.vector.tensor_tensor(bns[:, i:i + 1], bnr[:, i:i + 1], vec[:, 2 + 4 * i:3 + 4 * i], ALU.mult)
                last.then_inc(S["bn_scale"], 1)
                dve.wait_ge(S["bn_scale"], 1)
                for i in range(2):
                    last = nc.vector.tensor_tensor(bnr[:, i:i + 1], bns[:, i:i + 1], vec[:, 4 + 4 * i:5 + 4 * i], ALU.mult)
                last.then_inc(S["bn_scale"], 1)
                dve.wait_ge(S["bn_scale"], 2)
                for i in range(2):
                    last = nc.vector.tensor_tensor(bnb[:, i:i + 1], vec[:, 3 + 4 * i:4 + 4 * i], bnr[:, i:i + 1], ALU.subtract)
                nc.vector.tensor_scalar(bns_n[:], bns[:, 1:2], -1.0, None, ALU.mult)
                last.then_inc(S["bn_shift"], 1)

            def sum_taps():
                dve.wait_ge(S["loads_weights"], 11 * 16)
                taps = w_raw[:, W_CONV2:W_CONV2 + 2 * O_TAPS].rearrange("p (s two) o -> p s two o", two=2)
                nc.vector.tensor_tensor(w_raw[:, W_SUM:W_SUM + O_TAPS], taps[:, :, 0], taps[:, :, 1],
                                        ALU.add).then_inc(S["w_sum_made"], 1)

            def low_weights(part):
                w = slice(0, NW // 2) if part == 0 else slice(NW // 2, NW)
                dve.wait_ge(S["weights_hi"], 1)
                nc.vector.tensor_tensor(w_lo[:, w], w_raw[:, w], w_hi[:, w].bitcast(f32),
                                        ALU.subtract).then_inc(S["weights_split"], 1)

            def bn(src, st, sem):
                for g in range(G):
                    last = nc.vector.bn_stats(st[:, g], src[:, g])
                last.then_inc(sem, 1)

            def aggregate(st, mv, sem):
                dve.sem_inc(S["tick_dve"], 1)
                for g in range(G):
                    last = nc.vector.bn_aggr(mv[:, g], st[:, g])
                last.then_inc(sem, 1)

            def stats(src, st, mv, st_sem, mv_sem, n):
                bn(src, st, st_sem)
                dve.wait_ge(st_sem, n)
                aggregate(st, mv, mv_sem)
                dve.wait_ge(mv_sem, n)

            def body(k, u, s, prep, gcn, mid, conv, gate):
                p, q = s % 2, (s + 1) % 2
                if isinstance(k, int) and k == -2:
                    constants()
                if gate:
                    dve.wait_ge(S["conv2_done"], k)
                    dve.wait_ge(S["he_done"], k)
                    nc.vector.scalar_tensor_tensor(parity(cv, 0), CQ, bns[:, 1:2], he[:], ALU.mult, ALU.add)
                    dve.wait_ge(S["ho_done"], k)
                    nc.vector.scalar_tensor_tensor(ho[:], CQ, bns_n[:], ho[:], ALU.mult,
                                                   ALU.add).then_inc(S["hq_done"], 1)
                    dve.wait_ge(S["hq_done"], k)
                    nc.vector.scalar_tensor_tensor(parity(cv, 1), CR, bns[:, 1:2], ho[:], ALU.mult,
                                                   ALU.add).then_inc(S["cv_done"], 1)
                if conv:
                    dve.wait_ge(S["ht_hi_done"], k + 1)
                    wait(dve, S["gate_h_done"], k - 1)
                    nc.vector.tensor_tensor(ht_lo[:, p], ht[:, p], ht_hi[:, p].bitcast(f32),
                                            ALU.subtract).then_inc(S["ht_lo_done"], 1)
                if gate:
                    dve.wait_ge(S["xc_hi_done"], k)
                    nc.vector.scalar_tensor_tensor(xc_lo[:], cv[:], 0.0, xc_hi[:].bitcast(f32), ALU.max,
                                                   ALU.subtract).then_inc(S["xc_lo_done"], 1)
                if prep:
                    dve.wait_ge(adj_loaded[q], (u + 2 + p) * 16)
                    nc.vector.tensor_reduce(deg[:], adj_in[:, q], AX.X, ALU.add).then_inc(S["deg_done"], 1)
                    dve.wait_ge(S["deg_done"], k + 4)
                    nc.vector.tensor_scalar(deg0[:], deg[:], 0.0, None, ALU.is_equal).then_inc(S["deg0_done"], 1)
                    wait(dve, S["rsd_done"], k + 3)
                    nc.vector.tensor_scalar(pind[:, 0:4], deg[:], 1.0, DEG_EPS, ALU.add, ALU.add)
                    dve.wait_ge(S["deg0_done"], k + 4)
                    nc.vector.tensor_tensor(pind[:, 4:8], deg[:], deg0[:], ALU.add).then_inc(S["pind_done"], 1)
                if mid:
                    dve.wait_ge(S["spl_done"], k + 2)
                    nc.vector.scalar_tensor_tensor(sp[:], pre[:], 0.0, sp_l[:], ALU.max, ALU.add).then_inc(S["sp_done"], 1)
                    dve.wait_ge(S["sp_done"], k + 2)
                    wait(dve, S["x2b_done"], k + 1)
                    wait(dve, S["h2_done"], k + 1)
                    nc.vector.tensor_tensor(x2[:], x1[:], sp[:], ALU.add).then_inc(S["x2_done"], 1)
                    dve.wait_ge(S["x2_done"], k + 2)
                    stats(x2, st2, mv2, S["st2_done"], S["mv2_done"], k + 2)
                    nc.vector.tensor_scalar(pin2[:], mv2[:, :, 1], LN_EPS, None, ALU.add).then_inc(S["pin2_done"], 1)
                if gcn:
                    dve.wait_ge(S["w0_done"], k + 3)
                    wait(dve, S["a0_done"], k + 2)
                    for g in range(G):
                        last = nc.vector.scalar_tensor_tensor(y0[:, g], b0_bc[:], rsd[:, g:g + 1], XA[:, g],
                                                              ALU.mult, ALU.add)
                    last.then_inc(S["y0_done"], 1)
                if mid:
                    dve.wait_ge(S["rs2_done"], k + 2)
                    wait(dve, S["h2_done"], k + 1)
                    nc.vector.tensor_tensor(r2d[:], rs2[:], crs[:, q, 0:4], ALU.mult).then_inc(S["r2d_done"], 1)
                    dve.wait_ge(S["r2d_done"], k + 2)
                    nc.vector.scalar_tensor_tensor(nm2[:], mv2[:, :, 0], -1.0, r2d[:], ALU.mult,
                                                   ALU.mult).then_inc(S["nm2_done"], 1)
                if conv:
                    dve.wait_ge(S["c1_hi_done"], k + 1)
                    inner = slice(PAD // 2, PAD // 2 + HALF)
                    nc.vector.tensor_tensor(c1_lo[:, :, :, inner], c1[:, :, :, inner], c1_hi[:, :, :, inner].bitcast(f32),
                                            ALU.subtract).then_inc(S["c1_lo_done"], 1)
                    wait(dve, S["cs_lo_done"], k)
                    wait(dve, S["cs_hi_done"], k)
                    nc.vector.tensor_tensor(cs[:], c1[:, :, 1, 0:SROW], c1[:, :, 0, 1:SROW + 1],
                                            ALU.add).then_inc(S["cs_done"], 1)
                    dve.wait_ge(S["dl_s"], k + 1)
                    wait(dve, S["dist_done"], k)
                    nc.vector.tensor_scalar(dr[0:32], dl[0:32], 2.0, None, ALU.mult).then_inc(S["dr_s"], 1)
                if gcn:
                    dve.wait_ge(S["adj_t_done"], k + 3)
                    nc.vector.tensor_scalar(cs0[:], cin[:, 0:4], 0.0, None, ALU.is_equal).then_inc(S["cs0_done"], 1)
                    dve.wait_ge(S["cs0_done"], k + 3)
                    wait(dve, S["crs_done"], k + 2)
                    nc.vector.tensor_tensor(cin[:, 4:8], cin[:, 0:4], cs0[:], ALU.add).then_inc(S["cin_done"], 1)
                if isinstance(k, int) and k == -2:
                    sum_taps()
                if gcn:
                    dve.wait_ge(S["a0_done"], k + 3)
                    wait(dve, S["u0_done"], k + 2)
                    nc.vector.tensor_tensor(t0[:], XC[:], y0[:], ALU.add).then_inc(S["t0_done"], 1)
                    dve.wait_ge(S["t0_done"], k + 3)
                    dve.wait_ge(S["dm_done"], k + 3)
                    for g in range(G):
                        last = nc.vector.tensor_scalar(u0[:, g], t0[:, g], dm[:, g:g + 1], 0.0, ALU.mult, ALU.max)
                    last.then_inc(S["u0_done"], 1)
                    dve.wait_ge(S["u0_done"], k + 3)
                    dve.wait_ge(x_loaded[p], (u + 2) * 16)
                    wait(dve, S["x2_done"], k + 2)
                    wait(dve, S["c_done"], k + 2)
                    nc.vector.tensor_tensor(x1[:], x_in[:, p], u0[:], ALU.add).then_inc(S["x1_done"], 1)
                    dve.wait_ge(S["x1_done"], k + 3)
                    bn(x1, st1, S["st1_done"])
                    dve.wait_ge(S["crs_done"], k + 3)
                    nc.vector.scalar_tensor_tensor(ns_out[:], cs0[:], -1.0, crs[:, p, 4:8], ALU.add,
                                                   ALU.mult).then_inc(S["ns_done"], 1)
                    dve.wait_ge(S["st1_done"], k + 3)
                    aggregate(st1, mv1, S["mv1_done"])
                    dve.wait_ge(S["mv1_done"], k + 3)
                    nc.vector.tensor_scalar(e1[:], mv1[:, :, 1], LN_EPS, LN_EPS, ALU.add, ALU.mult).then_inc(S["e1_done"], 1)
                    wait(dve, S["z1_done"], k + 2)
                    for g in range(G):
                        last = nc.vector.tensor_scalar(cc[:, g], x1[:, g], mv1[:, g, 0:1], mv1[:, g, 0:1],
                                                       ALU.max, ALU.subtract)
                    last.then_inc(S["c_done"], 1)
                if gate:
                    dve.wait_ge(S["rz_done"], k)
                    nc.vector.scalar_tensor_tensor(rn[:], flat(GH[:]), vec[:, 15:16], rz[:, 0], ALU.add,
                                                   ALU.mult).then_inc(S["rn_done"], 1)
                    dve.wait_ge(S["rn_done"], k)
                    wait(dve, S["ne_done"], k - 1)
                    nc.vector.tensor_tensor(vn[:], flat(GI[:]), rn[:], ALU.add).then_inc(S["vn_done"], 1)
                if gcn:
                    dve.wait_ge(S["c_done"], k + 3)
                    stats(cc, stc, mvc, S["stc_done"], S["mvc_done"], k + 3)
                    dve.wait_ge(S["e1_done"], k + 3)
                    nc.vector.tensor_tensor(pin1[:], mvc[:, :, 1], e1[:], ALU.add).then_inc(S["pin1_done"], 1)
                if prep:
                    dve.wait_ge(x_loaded[q], (u + 2 + p) * 16)
                    bn(x_in[:, q], st0, S["st0_done"])
                if gate:
                    dve.wait_ge(S["nq_done"], k)
                    wait(dve, S["ot_done"], k - 1)
                    nc.vector.tensor_scalar(nn[:], nq[:], 2.0, -1.0, ALU.mult, ALU.add).then_inc(S["nn_done"], 1)
                if conv:
                    dve.wait_ge(S["cs_hi_done"], k + 1)
                    nc.vector.tensor_tensor(cs_lo[:], cs[:], cs_hi[:].bitcast(f32),
                                            ALU.subtract).then_inc(S["cs_lo_done"], 1)
                if gcn:
                    dve.wait_ge(S["q1_done"], k + 3)
                    nc.vector.scalar_tensor_tensor(nmq[:], mvc[:, :, 0], -1.0, q1[:], ALU.mult,
                                                   ALU.mult).then_inc(S["nmq_done"], 1)
                    dve.wait_ge(S["nmq_done"], k + 3)
                    wait(dve, S["z1t_psum"], k + 2)
                    for g in range(G // 2, G):
                        last = nc.vector.tensor_scalar(z1[:, g], cc[:, g], q1[:, g:g + 1], nmq[:, g:g + 1],
                                                       ALU.mult, ALU.add)
                    last.then_inc(S["z1b_done"], 1)
                if isinstance(k, int) and k in (-2, -1):
                    low_weights(k + 2)
                if mid:
                    dve.wait_ge(S["w2_done"], k + 2)
                    dve.wait_ge(S["x2b_done"], k + 2)
                    wait(dve, S["x4_done"], k - 2)
                    for g in range(G):
                        last = nc.vector.scalar_tensor_tensor(x3[:, (s + 1) % 4, g], XC[:, g], crs[:, q, g:g + 1],
                                                              x2b[:, g], ALU.mult, ALU.add)
                    last.then_inc(S["x3_done"], 1)
                if prep:
                    dve.wait_ge(S["st0_done"], k + 4)
                    aggregate(st0, mv0, S["mv0_done"])
                if mid:
                    dve.wait_ge(S["x3_done"], k + 2)
                    bn(x3[:, (s + 1) % 4], st3, S["st3_done"])
                if prep:
                    dve.wait_ge(S["mv0_done"], k + 4)
                    wait(dve, S["rs0_done"], k + 3)
                    nc.vector.tensor_scalar(pin0[:], mv0[:, :, 1], LN_EPS, None, ALU.add).then_inc(S["pin0_done"], 1)
                if mid:
                    dve.wait_ge(S["st3_done"], k + 2)
                    aggregate(st3, mv3, S["mv3_done"])
                    dve.wait_ge(S["mv3_done"], k + 2)
                    nc.vector.tensor_scalar(pin3[:], mv3[:, :, 1], LN_EPS, None, ALU.add).then_inc(S["pin3_done"], 1)
                if gcn:
                    dve.wait_ge(S["w1n_done"], k + 3)
                    wait(dve, S["a1_done"], k + 2)
                    nc.vector.tensor_tensor(y1[:], XA[:], s_in[:, p].unsqueeze(2).broadcast_to([P, G, P]),
                                            ALU.mult).then_inc(S["y1_done"], 1)
                if conv:
                    dve.wait_ge(S["xn_hi_done"], k + 1)
                    nc.vector.tensor_tensor(xn_lo[:], GI[:], xn_hi[:].bitcast(f32), ALU.subtract).then_inc(S["xn_lo_done"], 1)
                if mid:
                    dve.wait_ge(S["rs3_done"], k + 2)
                    wait(dve, S["xh3_done"], k + 1)
                    nc.vector.scalar_tensor_tensor(nm3[:], mv3[:, :, 0], -1.0, rs3[:], ALU.mult,
                                                   ALU.mult).then_inc(S["nm3_done"], 1)
                if prep:
                    dve.wait_ge(S["rs0_done"], k + 4)
                    dve.wait_ge(S["rsd_done"], k + 4)
                    wait(dve, S["xh0_done"], k + 3)
                    nc.vector.tensor_tensor(r0d[:], rs0[:], rsd[:, 0:4], ALU.mult).then_inc(S["r0d_done"], 1)
                    nc.vector.tensor_scalar(deg0[:], deg0[:], -1.0, 1.0, ALU.mult, ALU.add).then_inc(S["is0_done"], 1)
                    dve.wait_ge(S["r0d_done"], k + 4)
                    nc.vector.scalar_tensor_tensor(nm0[:], mv0[:, :, 0], -1.0, r0d[:], ALU.mult,
                                                   ALU.mult).then_inc(S["nm0_done"], 1)
                    dve.wait_ge(S["is0_done"], k + 4)
                    nc.vector.tensor_tensor(s_in[:, q], rsd[:, 4:8], deg0[:], ALU.mult)
                    mask_cols = mask_sb[:, bass.ds((k + 3) * G, G)] if not isinstance(k, int) else \
                        mask_sb[:, (k + 3) * G:(k + 4) * G]
                    wait(dve, S["u0_done"], k + 3)
                    if isinstance(k, int) and k == -3:
                        dve.wait_ge(S["loads_consts"], 9 * 16)
                    nc.vector.tensor_tensor(dm[:], rsd[:, 0:4], mask_cols, ALU.mult).then_inc(S["dm_done"], 1)
                if gcn:
                    dve.wait_ge(S["a1_done"], k + 3)
                    dve.wait_ge(S["self1_done"], k + 3)
                    dve.wait_ge(S["ns_done"], k + 3)
                    wait(dve, S["spa_done"], k + 2)
                    for g in range(G):
                        last = nc.vector.scalar_tensor_tensor(pre[:, g], XC[:, g], ns_out[:, g:g + 1], self1[:, g],
                                                              ALU.mult, ALU.add)
                    last.then_inc(S["pre_done"], 1)
                if gate:
                    dve.wait_ge(S["ot_psum"], k)
                    if not isinstance(k, int) or u - 1 + p > 0:
                        dve.wait_ge(x_stored[q], (u - 1 + p) * 16)
                    nc.vector.tensor_tensor(x4[:, q], XB[:], x3[:, (s + 3) % 4], ALU.add).then_inc(S["x4_done"], 1)

            steps(dve, body)

        @block.tensor
        def _(pe):
            def transposes(dst, src):
                for g in range(G):
                    last = nc.tensor.transpose(dst[:, g], src[:, g], ident[:])
                return last

            def per_graph(dst, lhs, rhs):
                for g in range(G):
                    last = nc.tensor.matmul(dst[:, g], lhs(g), rhs(g), start=True, stop=True)
                return last

            def split_product(dst, w, hi, lo, start, stop):
                nc.tensor.matmul(dst, w_hi[:, w], hi, start=start, stop=False)
                nc.tensor.matmul(dst, w_hi[:, w], lo, start=False, stop=False)
                return nc.tensor.matmul(dst, w_lo[:, w], hi, start=False, stop=stop)

            def taps_p(first, last_tap):
                for t in range(first, last_tap):
                    last = split_product(CP, W_CONV2 + 2 * t, c1_hi[:, :, 0, t:t + HALF + 2],
                                         c1_lo[:, :, 0, t:t + HALF + 2], t == 0, t == E_TAPS - 1)
                return last

            def taps_q(first, last_tap):
                for t in range(first, last_tap):
                    last = split_product(CQ, W_CONV2 + 2 * t + 1, c1_hi[:, :, 1, t:t + HALF],
                                         c1_lo[:, :, 1, t:t + HALF], t == 0, t == O_TAPS - 1)
                return last

            def taps_r(first, last_tap):
                for t in range(first, last_tap):
                    last = split_product(CR, W_SUM + t if t < O_TAPS else W_CONV2 + TAPS - 1,
                                         cs_hi[:, :, t:t + HALF], cs_lo[:, :, t:t + HALF], t == 0, t == E_TAPS - 1)
                return last

            def body(k, u, s, prep, gcn, mid, conv, gate):
                p, q = s % 2, (s + 1) % 2
                if isinstance(k, int) and k == -2:
                    pe.wait_ge(S["ident_made"], 1)
                    pe.wait_ge(S["loads_consts"], 9 * 16)
                    pe.wait_ge(S["w1_sum"], 1)
                if isinstance(k, int) and k == 0:
                    pe.wait_ge(S["weights_split"], 2)
                    pe.wait_ge(S["bm3_made"], 1)
                if conv:
                    pe.wait_ge(S["xh3_done"], k + 1)
                    wait(pe, S["y1_done"], k + 2)
                    transposes(XA, xh3).then_inc(S["ht_psum"], 1)
                if gate:
                    wait(pe, S["z2t_done"], k + 1)
                    wait(pe, S["gez_done"], k - 1)
                    wait(pe, S["self1_done"], k + 2)
                    hi, lo = ht_hi[:, q], ht_lo[:, q]
                    split_product(GR[:], W_HH, hi, lo, True, False)
                    split_product(GZ[:], W_HH + 1, hi, lo, True, False)
                    split_product(GH[:], W_HH + 2, hi, lo, True, True).then_inc(S["gate_h_done"], 1)
                if gcn:
                    pe.wait_ge(adj_loaded[p], (u + 2) * 16)
                    wait(pe, S["x3_done"], k + 1)
                    wait(pe, S["pre_done"], k + 2)
                    transposes(XC, adj_in[:, p]).then_inc(S["adj_t_psum"], 1)
                    pe.wait_ge(S["xh0_done"], k + 3)
                    wait(pe, S["ht_hi_done"], k + 1)
                    wait(pe, S["y1_done"], k + 2)
                    transposes(XA, xh0).then_inc(S["h0t_psum"], 1)
                if gate:
                    pe.wait_ge(S["xn_lo_done"], k)
                    for i, dst in enumerate((GR, GZ, GI)):
                        split_product(dst[:], W_IH + 3 + i, xn_hi[:], xn_lo[:], i == 2, False)
                if gcn:
                    pe.wait_ge(S["h0t_done"], k + 3)
                    per_graph(XA, lambda g: h0t[:, g], lambda g: w0[:]).then_inc(S["w0_done"], 1)
                if conv:
                    pe.wait_ge(S["ht_lo_done"], k + 1)
                    wait(pe, S["cv_done"], k)
                    split_product(CB[:], W_CONV1, ht_hi[:, p], ht_lo[:, p], True, True).then_inc(S["conv1_done"], 1)
                    wait(pe, S["x4_done"], k - 1)
                    split_product(XB[:], W_SE, ht_hi[:, p], ht_lo[:, p], True, True).then_inc(S["se_done"], 1)
                if gate:
                    pe.wait_ge(S["xc_lo_done"], k)
                    for i, dst in enumerate((GR, GZ, GI)):
                        last = split_product(dst[:], W_IH + i, xc_hi[:], xc_lo[:], False, True)
                    last.then_inc(S["gates_done"], 1)
                if gcn:
                    pe.wait_ge(S["y0_done"], k + 3)
                    pe.wait_ge(S["adj_t_done"], k + 3)
                    per_graph(XC, lambda g: adj_t[:, (s + 2) % 4, g], lambda g: y0[:, g]).then_inc(S["a0_done"], 1)
                if conv:
                    pe.wait_ge(S["c1_lo_done"], k + 1)
                    taps_p(0, 4)
                    wait(pe, S["ge_done"], k)
                    nc.tensor.matmul(GR[:], ones[:], bm3[:], start=True, stop=True, skip_group_check=True)
                    for g in range(G):
                        last = nc.tensor.matmul(GR[:, g], ht[:, p, g], w_raw[:, W_MSG], start=False, stop=True,
                                                skip_group_check=True)
                    last.then_inc(S["msg_psum"], 1)
                    taps_p(4, E_TAPS).then_inc(S["convp_done"], 1)
                    for name in ("dl_s", "dr_s", "dl_q", "dr_q"):
                        pe.wait_ge(S[name], k + 1)
                    per_graph(XB, lambda g: dl[:, g], lambda g: dr[:, g]).then_inc(S["dist_done"], 1)
                if mid:
                    pe.wait_ge(S["h2_done"], k + 2)
                    wait(pe, S["msg_done"], k + 1)
                    wait(pe, S["z2t_done"], k + 1)
                    per_graph(GR, lambda g: h2[:, g], lambda g: adj_t[:, (s + 1) % 4, g]).then_inc(S["a2_done"], 1)
                if conv:
                    pe.wait_ge(S["pe_done"], k + 1)
                    taps_q(0, O_TAPS)
                if mid:
                    pe.wait_ge(S["z2t_done"], k + 2)
                    wait(pe, S["t0_done"], k + 3)
                    per_graph(XC, lambda g: z2t[:, g], lambda g: w2_sb[:]).then_inc(S["w2_done"], 1)
                if conv:
                    pe.wait_ge(S["m3_done"], k + 1)
                    pe.wait_ge(S["msg_done"], k + 1)
                    wait(pe, S["vn_done"], k)
                    per_graph(GI, lambda g: msg[:, g], lambda g: m3[:, g]).then_inc(S["a3_done"], 1)
                    pe.wait_ge(S["cs_lo_done"], k + 1)
                    taps_r(0, 2)
                if gcn:
                    pe.wait_ge(S["z1_done"], k + 3)
                    pe.wait_ge(S["z1b_done"], k + 3)
                    transposes(XA, z1).then_inc(S["z1t_psum"], 1)
                if conv:
                    taps_r(2, 5)
                if gcn:
                    pe.wait_ge(S["z1t_done"], k + 3)
                    wait(pe, S["rn_done"], k)
                    wait(pe, S["self1_done"], k + 2)
                    per_graph(XA, lambda g: z1t[:, g], lambda g: w1n[:]).then_inc(S["w1n_done"], 1)
                    per_graph(GH, lambda g: z1t[:, g], lambda g: w1ns[:]).then_inc(S["w1_done"], 1)
                if conv:
                    taps_r(5, 7)
                if gcn:
                    pe.wait_ge(S["y1_done"], k + 3)
                    wait(pe, S["x3_done"], k + 2)
                    wait(pe, S["t0_done"], k + 3)
                    per_graph(XC, lambda g: adj_t[:, (s + 2) % 4, g], lambda g: y1[:, g]).then_inc(S["a1_done"], 1)
                if conv:
                    taps_r(7, E_TAPS).then_inc(S["conv2_done"], 1)
                if gate:
                    pe.wait_ge(S["ot_done"], k)
                    wait(pe, S["ex_done"], k + 1)
                    wait(pe, S["x4_done"], k - 1)
                    transposes(XB, ot).then_inc(S["ot_psum"], 1)

            steps(pe, body)


def kernel(**inputs):
    import numpy as np
    import concourse.bacc as bacc
    from concourse.bass_utils import run_bass_kernel_spmd

    a = {n: np.asarray(v) for n, v in inputs.items()}
    w3 = {n[len("L3_gnn_"):]: v for n, v in a.items() if n.startswith("L3_gnn_")}
    b_ih, b_hh = w3["b_ih"].reshape(3, P), w3["b_hh"].reshape(3, P)
    vecs = np.stack([a["L1_gnn_gamma"], a["L1_gnn_beta"],
                     w3["bn1_g"], w3["bn1_b"], w3["bn1_m"], w3["bn1_v"],
                     w3["bn2_g"], w3["bn2_b"], w3["bn2_m"], w3["bn2_v"],
                     b_ih[0], b_ih[1], b_ih[2], b_hh[0], b_hh[1], b_hh[2]], axis=1)
    arrays = {
        "x": a["x"], "adj": a["adj"], "mask_t": a["nodemask"].T,
        "w0_t": a["L0_gnn_W"].T, "w1_self": a["L1_gnn_W_self"], "w1_neigh": a["L1_gnn_W_neigh"],
        "w2": a["L2_gnn_weight"],
        "conv2_t": w3["conv2_w"].transpose(1, 2, 0),
        "conv1_t": w3["conv1_w"][:, :, 0].T, "msg_t": w3["w_msg"].T, "se_t": w3["w_se"].T,
        "ih_t": w3["w_ih"].reshape(3, P, 2, P).transpose(3, 2, 0, 1).reshape(P, 6, P),
        "hh_t": w3["w_hh"].reshape(3, P, P).transpose(2, 0, 1),
        "vecs": vecs, "b_se": w3["b_se"].reshape(3, 1),
        "rows": np.stack([a["L0_gnn_b"], a["L2_gnn_bias"], w3["b_msg"]]),
    }
    arrays = {n: np.ascontiguousarray(v) for n, v in arrays.items()}
    nc = bacc.Bacc("TRN2", target_bir_lowering=False, num_devices=1)
    args = [nc.dram_tensor(f"in_{n}", v.shape, mybir.dt.from_np(v.dtype), kind="ExternalInput").ap()
            for n, v in arrays.items()]
    args.append(nc.dram_tensor("out_0", (GRAPHS, P, P), mybir.dt.float32, kind="ExternalOutput").ap())
    graph_net(nc, *args)
    r = run_bass_kernel_spmd(nc, [{f"in_{n}": v for n, v in arrays.items()}], core_ids=[0])
    return r.results[0]["out_0"]
```
